# Optimizing a Trainium2 kernel written in Bass

```python
import numpy as np
import jax
import jax.numpy as jnp

def _softmax(x, axis=-1):
    return jax.nn.softmax(x, axis=axis)

def _gelu(x):
    return jax.nn.gelu(x, approximate=True)

def _silu(x):
    return jax.nn.silu(x)

def _sigmoid(x):
    return jax.nn.sigmoid(x)

def _layernorm(x, axis=-1, eps=1e-05):
    m = jnp.mean(x, axis=axis, keepdims=True)
    v = jnp.var(x, axis=axis, keepdims=True)
    return (x - m) / jnp.sqrt(v + eps)

def _scatter_add(tgt, idx, src, axis=0):
    return tgt.at[idx].add(src)

def _segment_sum(src, seg, n):
    return jax.ops.segment_sum(src, seg, n)
kernel_name = 'mk_flamingo_gated_d4_seqx_r8_562bd7'

def setup_inputs(seed: int=0):
    np.random.seed(seed)
    _w = jnp.asarray

    def _rec_inputs():
        import jax
        import jax.numpy as jnp
        _rk = jax.random.key(seed)
        x = 7.22e-05 + 1 * jax.random.normal(jax.random.fold_in(_rk, 1), (32, 64, 512), jnp.float32)
        _lenS = 64 - jax.random.randint(jax.random.fold_in(_rk, 7), (32,), 0, max(1, 64 // 4) + 1, jnp.int32)
        _lenS2 = 64 - jax.random.randint(jax.random.fold_in(_rk, 8), (32,), 0, max(1, 64 // 4) + 1, jnp.int32)
        _ctx_4096P = jax.random.normal(jax.random.fold_in(_rk, 11), (32, 16, 512), jnp.float32)
        _ctx_4096c = jax.random.dirichlet(jax.random.fold_in(_rk, 511), 0.3 * jnp.ones((16,), jnp.float32), (32, 64))
        _ctx_4096t = jnp.einsum('bsk,bkd->bsd', _ctx_4096c, _ctx_4096P)
        _ctx_4096t = _ctx_4096t * jax.lax.rsqrt(jnp.mean(jnp.square(_ctx_4096t)) + 1e-12) * 0.953939
        ctx_4096 = 4.13588e-05 + 0.999923 * (_ctx_4096t + 0.3 * jax.random.normal(jax.random.fold_in(_rk, 611), (32, 64, 512), jnp.float32))
        _validS = jnp.arange(64)[None, :] < _lenS[:, None]
        _validS2 = jnp.arange(64)[None, :] < _lenS2[:, None]
        _causal = jnp.tril(jnp.ones((64, 64), dtype=bool))
        mask_1x1xSxS2_ff0 = jnp.where(jnp.ones((1, 1, 64, 64), dtype=bool), 0.0, -1000000000.0).astype(jnp.float32)
        _g = jax.random.normal(jax.random.fold_in(_rk, 9001), (2, 4), jnp.float32)
        _g = jnp.sign(_g) * jnp.maximum(jnp.abs(_g), 1.0) + (_g == 0) * 1.0
        g_xattn = _g[0]
        g_ffn = _g[1]
        return (x, ctx_4096, mask_1x1xSxS2_ff0, g_xattn, g_ffn)
    x, ctx_4096, mask_1x1xSxS2_ff0, g_xattn, g_ffn = _rec_inputs()

    def _L0_xattn_setup():
        import jax, jax.numpy as jnp
        import numpy as np
        HEADS = 8
        WINDOW = 16

        def _pointwise(W, b, t):
            return jnp.einsum('oc,bct->bot', W, t) + b[None, :, None]
        key = jax.random.key(seed)
        ks = jax.random.split(key, 10)
        B, C, T = (4, 64, 512)
        s = 0.02
        return {'x': jax.random.normal(ks[0], (B, C, T), jnp.float32), 'cond': jax.random.normal(ks[1], (B, C, T), jnp.float32), 'Wq': jax.random.normal(ks[2], (C, C), jnp.float32) * s, 'bq': jnp.zeros((C,), jnp.float32), 'Wk': jax.random.normal(ks[3], (C, C), jnp.float32) * s, 'bk': jnp.zeros((C,), jnp.float32), 'Wv': jax.random.normal(ks[4], (C, C), jnp.float32) * s, 'bv': jnp.zeros((C,), jnp.float32), 'Wo': jax.random.normal(ks[5], (C, C), jnp.float32) * s, 'bo': jnp.zeros((C,), jnp.float32)}
    _L0_xattn_all = _L0_xattn_setup()
    _L0_xattn_in = {k: v for k, v in _L0_xattn_all.items() if k in ('Wq', 'bq', 'Wk', 'bk', 'Wv', 'bv', 'Wo', 'bo')}
    del _L0_xattn_all

    def _L0_ffn_setup():
        import jax, jax.numpy as jnp
        import numpy as np
        NUM_EXPERTS = 8
        TOP_K = 2
        RANK = 16
        LORA_ALPHA = 32
        SCALING = LORA_ALPHA / RANK
        key = jax.random.key(seed)
        ks = jax.random.split(key, 6)
        B, S, D_IN, D_OUT = (4, 256, 512, 512)
        x = jax.random.normal(ks[0], (B, S, D_IN), dtype=jnp.float32)
        W_base = jax.random.normal(ks[1], (D_OUT, D_IN), dtype=jnp.float32) * 0.02
        b_base = jax.random.normal(ks[2], (D_OUT,), dtype=jnp.float32) * 0.02
        W_router = jax.random.normal(ks[3], (NUM_EXPERTS, D_IN), dtype=jnp.float32) * 0.02
        A = jax.random.normal(ks[4], (NUM_EXPERTS, RANK, D_IN), dtype=jnp.float32) * 0.02
        Bm = jax.random.normal(ks[5], (D_OUT, RANK), dtype=jnp.float32) * 0.02
        Bm = jnp.broadcast_to(Bm, (NUM_EXPERTS, D_OUT, RANK)) * jnp.arange(1, NUM_EXPERTS + 1, dtype=jnp.float32)[:, None, None] * 0.2
        return {'x': x, 'W_base': W_base, 'b_base': b_base, 'W_router': W_router, 'A': A, 'B': Bm}
    _L0_ffn_all = _L0_ffn_setup()
    _L0_ffn_in = {k: v for k, v in _L0_ffn_all.items() if k in ('W_base', 'b_base', 'W_router', 'A', 'B')}
    del _L0_ffn_all

    def _L1_xattn_setup():
        import jax, jax.numpy as jnp
        import numpy as np
        import math
        HIDDEN = 512
        N_HEADS = 32
        HEAD_DIM = 128
        N_KV_HEADS = 4
        N_GROUPS = N_HEADS // N_KV_HEADS
        key = jax.random.key(seed)
        ks = jax.random.split(key, 6)
        B, NL, S = (8, 64, 512)
        latents = jax.random.normal(ks[0], (B, NL, HIDDEN), dtype=jnp.float32)
        context = jax.random.normal(ks[1], (B, S, HIDDEN), dtype=jnp.float32)
        scale = 1.0 / math.sqrt(HIDDEN)
        Wq = jax.random.normal(ks[2], (HIDDEN, N_HEADS * HEAD_DIM), dtype=jnp.float32) * scale
        Wk = jax.random.normal(ks[3], (HIDDEN, N_KV_HEADS * HEAD_DIM), dtype=jnp.float32) * scale
        Wv = jax.random.normal(ks[4], (HIDDEN, N_KV_HEADS * HEAD_DIM), dtype=jnp.float32) * scale
        Wo = jax.random.normal(ks[5], (N_HEADS * HEAD_DIM, HIDDEN), dtype=jnp.float32) * scale
        return {'latents': latents, 'context': context, 'Wq': Wq, 'Wk': Wk, 'Wv': Wv, 'Wo': Wo}
    _L1_xattn_all = _L1_xattn_setup()
    _L1_xattn_in = {k: v for k, v in _L1_xattn_all.items() if k in ('Wq', 'Wk', 'Wv', 'Wo')}
    del _L1_xattn_all

    def _L1_ffn_setup():
        import jax, jax.numpy as jnp
        import numpy as np
        MAX_THRESHOLD = 1.0 / 8.0
        SCALING = 32.0 / 16.0
        key = jax.random.key(seed)
        ks = jax.random.split(key, 8)
        B_, S, D, O, E, R = (4, 256, 512, 512, 8, 16)
        sd = 1.0 / np.sqrt(D)
        return {'x': jax.random.normal(ks[0], (B_, S, D), jnp.float32), 'W_base': jax.random.normal(ks[1], (O, D), jnp.float32) * sd, 'b_base': jax.random.normal(ks[2], (O,), jnp.float32) * 0.01, 'W_gate': jax.random.normal(ks[3], (E, D), jnp.float32) * sd, 'W_thr': jax.random.normal(ks[4], (1, D), jnp.float32) * sd, 'b_thr': jax.random.normal(ks[5], (1,), jnp.float32) * 0.01, 'A': jax.random.normal(ks[6], (E, R, D), jnp.float32) * sd, 'B': jax.random.normal(ks[7], (O,), jnp.float32)[None, :, None] * jnp.zeros((E, O, R), jnp.float32) + jax.random.normal(jax.random.fold_in(key, 7), (E, O, R), jnp.float32) * (1.0 / np.sqrt(R))}
    _L1_ffn_all = _L1_ffn_setup()
    _L1_ffn_in = {k: v for k, v in _L1_ffn_all.items() if k in ('W_base', 'b_base', 'W_gate', 'W_thr', 'b_thr', 'A', 'B')}
    del _L1_ffn_all

    def _L2_xattn_setup():
        import jax, jax.numpy as jnp
        import numpy as np
        TEXT_DIM = 512
        FEATURE_DIM = 512

        def _xavier_uniform(key, shape):
            fan_in, fan_out = (shape[1], shape[0])
            limit = float(np.sqrt(6.0 / (fan_in + fan_out)))
            return jax.random.uniform(key, shape, jnp.float32, -limit, limit)
        key = jax.random.key(seed)
        k1, k2, k3, k4 = jax.random.split(key, 4)
        text = jax.random.normal(k1, (8, 256, TEXT_DIM), jnp.float32)
        features = jax.random.normal(k2, (8, 72, FEATURE_DIM), jnp.float32)
        Wq = _xavier_uniform(k3, (FEATURE_DIM, TEXT_DIM))
        bq = jnp.zeros((FEATURE_DIM,), jnp.float32)
        Wk = _xavier_uniform(k4, (FEATURE_DIM, FEATURE_DIM))
        bk = jnp.zeros((FEATURE_DIM,), jnp.float32)
        return {'text': text, 'features': features, 'Wq': Wq, 'bq': bq, 'Wk': Wk, 'bk': bk}
    _L2_xattn_all = _L2_xattn_setup()
    _L2_xattn_in = {k: v for k, v in _L2_xattn_all.items() if k in ('Wq', 'bq', 'Wk', 'bk')}
    del _L2_xattn_all

    def _L2_ffn_setup():
        import jax, jax.numpy as jnp
        import numpy as np
        EPS = 1e-05

        def rms_norm(x):
            return x * jax.lax.rsqrt(jnp.mean(x * x, axis=-1, keepdims=True) + EPS)

        def activation_quant(x):
            scale = 127.0 / jnp.clip(jnp.max(jnp.abs(x), axis=-1, keepdims=True), EPS, None)
            return jnp.clip(jnp.round(x * scale), -128.0, 127.0) / scale

        def weight_quant(w):
            scale = 1.0 / jnp.clip(jnp.mean(jnp.abs(w)), EPS, None)
            return jnp.clip(jnp.round(w * scale), -1.0, 1.0) / scale
        key = jax.random.key(seed)
        k1, k2, k3 = jax.random.split(key, 3)
        B, S, D = (4, 256, 512)
        x = jax.random.normal(k1, (B, S, D), dtype=jnp.float32)
        W = jax.random.normal(k2, (D, D), dtype=jnp.float32) * (1.0 / np.sqrt(D))
        b = jax.random.normal(k3, (D,), dtype=jnp.float32) * 0.02
        return {'x': x, 'W': W, 'b': b}
    _L2_ffn_all = _L2_ffn_setup()
    _L2_ffn_in = {k: v for k, v in _L2_ffn_all.items() if k in ('W', 'b')}
    del _L2_ffn_all

    def _L3_xattn_setup():
        import jax, jax.numpy as jnp
        import numpy as np
        B, Q, K, D = (1, 128, 6404, 512)
        H, KVH, HD = (32, 8, 128)
        GROUPS = H // KVH
        EPS = 1e-05

        def _rmsnorm(x, w):
            xf = x.astype(jnp.float32)
            var = jnp.mean(xf * xf, axis=-1, keepdims=True)
            return (xf * jax.lax.rsqrt(var + EPS)).astype(x.dtype) * w
        key = jax.random.key(seed)
        ks = jax.random.split(key, 8)
        s = 0.02
        return {'hidden_states': jax.random.normal(ks[0], (B, Q, D), jnp.float32), 'cross_attention_states': jax.random.normal(ks[1], (B, K, D), jnp.float32), 'attention_mask': jnp.zeros((B, 1, Q, K), jnp.float32), 'Wq': jax.random.normal(ks[2], (H * HD, D), jnp.float32) * s, 'Wk': jax.random.normal(ks[3], (KVH * HD, D), jnp.float32) * s, 'Wv': jax.random.normal(ks[4], (KVH * HD, D), jnp.float32) * s, 'Wo': jax.random.normal(ks[5], (D, H * HD), jnp.float32) * s, 'q_norm_w': jnp.ones((HD,), jnp.float32), 'k_norm_w': jnp.ones((HD,), jnp.float32)}
    _L3_xattn_all = _L3_xattn_setup()
    _L3_xattn_in = {k: v for k, v in _L3_xattn_all.items() if k in ('Wq', 'Wk', 'Wv', 'Wo', 'q_norm_w', 'k_norm_w')}
    del _L3_xattn_all

    def _L3_ffn_setup():
        import jax, jax.numpy as jnp
        import numpy as np
        ALPHA = 32
        R = 16
        SCALING = ALPHA / R
        key = jax.random.key(seed)
        k1, k2, k3, k4 = jax.random.split(key, 4)
        B_, S, D = (4, 256, 512)
        H, r, O = (8, R, 512)
        x = jax.random.normal(k1, (B_, S, D), dtype=jnp.float32)
        A = jax.random.normal(k2, (H, r, D), dtype=jnp.float32) * 0.02
        Bm = jax.random.normal(k3, (H, O, r), dtype=jnp.float32) * 0.02
        Wr = jax.random.normal(k4, (H, D), dtype=jnp.float32) * 0.02
        br = jnp.zeros((H,), dtype=jnp.float32)
        return {'x': x, 'A': A, 'B': Bm, 'Wr': Wr, 'br': br}
    _L3_ffn_all = _L3_ffn_setup()
    _L3_ffn_in = {k: v for k, v in _L3_ffn_all.items() if k in ('A', 'B', 'Wr', 'br')}
    del _L3_ffn_all
    return {'x': x, 'ctx_4096': ctx_4096, 'mask_1x1xSxS2_ff0': mask_1x1xSxS2_ff0, 'g_xattn': g_xattn, 'g_ffn': g_ffn, 'L0_xattn_Wq': _L0_xattn_in['Wq'], 'L0_xattn_bq': _L0_xattn_in['bq'], 'L0_xattn_Wk': _L0_xattn_in['Wk'], 'L0_xattn_bk': _L0_xattn_in['bk'], 'L0_xattn_Wv': _L0_xattn_in['Wv'], 'L0_xattn_bv': _L0_xattn_in['bv'], 'L0_xattn_Wo': _L0_xattn_in['Wo'], 'L0_xattn_bo': _L0_xattn_in['bo'], 'L0_ffn_W_base': _L0_ffn_in['W_base'], 'L0_ffn_b_base': _L0_ffn_in['b_base'], 'L0_ffn_W_router': _L0_ffn_in['W_router'], 'L0_ffn_A': _L0_ffn_in['A'], 'L0_ffn_B': _L0_ffn_in['B'], 'L1_xattn_Wq': _L1_xattn_in['Wq'], 'L1_xattn_Wk': _L1_xattn_in['Wk'], 'L1_xattn_Wv': _L1_xattn_in['Wv'], 'L1_xattn_Wo': _L1_xattn_in['Wo'], 'L1_ffn_W_base': _L1_ffn_in['W_base'], 'L1_ffn_b_base': _L1_ffn_in['b_base'], 'L1_ffn_W_gate': _L1_ffn_in['W_gate'], 'L1_ffn_W_thr': _L1_ffn_in['W_thr'], 'L1_ffn_b_thr': _L1_ffn_in['b_thr'], 'L1_ffn_A': _L1_ffn_in['A'], 'L1_ffn_B': _L1_ffn_in['B'], 'L2_xattn_Wq': _L2_xattn_in['Wq'], 'L2_xattn_bq': _L2_xattn_in['bq'], 'L2_xattn_Wk': _L2_xattn_in['Wk'], 'L2_xattn_bk': _L2_xattn_in['bk'], 'L2_ffn_W': _L2_ffn_in['W'], 'L2_ffn_b': _L2_ffn_in['b'], 'L3_xattn_Wq': _L3_xattn_in['Wq'], 'L3_xattn_Wk': _L3_xattn_in['Wk'], 'L3_xattn_Wv': _L3_xattn_in['Wv'], 'L3_xattn_Wo': _L3_xattn_in['Wo'], 'L3_xattn_q_norm_w': _L3_xattn_in['q_norm_w'], 'L3_xattn_k_norm_w': _L3_xattn_in['k_norm_w'], 'L3_ffn_A': _L3_ffn_in['A'], 'L3_ffn_B': _L3_ffn_in['B'], 'L3_ffn_Wr': _L3_ffn_in['Wr'], 'L3_ffn_br': _L3_ffn_in['br']}

def reference(x, ctx_4096, mask_1x1xSxS2_ff0, g_xattn, g_ffn, L0_xattn_Wq, L0_xattn_bq, L0_xattn_Wk, L0_xattn_bk, L0_xattn_Wv, L0_xattn_bv, L0_xattn_Wo, L0_xattn_bo, L0_ffn_W_base, L0_ffn_b_base, L0_ffn_W_router, L0_ffn_A, L0_ffn_B, L1_xattn_Wq, L1_xattn_Wk, L1_xattn_Wv, L1_xattn_Wo, L1_ffn_W_base, L1_ffn_b_base, L1_ffn_W_gate, L1_ffn_W_thr, L1_ffn_b_thr, L1_ffn_A, L1_ffn_B, L2_xattn_Wq, L2_xattn_bq, L2_xattn_Wk, L2_xattn_bk, L2_ffn_W, L2_ffn_b, L3_xattn_Wq, L3_xattn_Wk, L3_xattn_Wv, L3_xattn_Wo, L3_xattn_q_norm_w, L3_xattn_k_norm_w, L3_ffn_A, L3_ffn_B, L3_ffn_Wr, L3_ffn_br):
    import jax
    import jax.numpy as jnp

    def _L0_xattn_ref(x, cond, Wq, bq, Wk, bk, Wv, bv, Wo, bo):
        import jax, jax.numpy as jnp
        import numpy as np
        HEADS = 8
        WINDOW = 16

        def _pointwise(W, b, t):
            return jnp.einsum('oc,bct->bot', W, t) + b[None, :, None]
        B, C, T = x.shape
        H, W = (HEADS, WINDOW)
        hd = C // H
        scale = hd ** (-0.5)
        pad_left = W // 2
        pad_right = W - pad_left - 1
        q = _pointwise(Wq, bq, x)
        k = _pointwise(Wk, bk, cond)
        v = _pointwise(Wv, bv, cond)
        k = jnp.pad(k, ((0, 0), (0, 0), (pad_left, pad_right)))
        v = jnp.pad(v, ((0, 0), (0, 0), (pad_left, pad_right)))
        idx = jnp.arange(T)[:, None] + jnp.arange(W)[None, :]
        k_win = k[:, :, idx].reshape(B, H, hd, T, W)
        v_win = v[:, :, idx].reshape(B, H, hd, T, W)
        qh = q.reshape(B, H, hd, T)
        dots = jnp.einsum('bhdt,bhdtw->bhtw', qh, k_win) * scale
        attn = jax.nn.softmax(dots, axis=-1)
        out = jnp.einsum('bhtw,bhdtw->bhdt', attn, v_win)
        out = out.reshape(B, C, T)
        return _pointwise(Wo, bo, out)

    def _L0_ffn_ref(x, W_base, b_base, W_router, A, B):
        import jax, jax.numpy as jnp
        import numpy as np
        NUM_EXPERTS = 8
        TOP_K = 2
        RANK = 16
        LORA_ALPHA = 32
        SCALING = LORA_ALPHA / RANK
        bs, seq, d_in = x.shape
        T = bs * seq
        xf = x.reshape(T, d_in)
        base = xf @ W_base.T + b_base
        logits = xf @ W_router.T
        rw, sel = jax.lax.top_k(logits, TOP_K)
        rw = jax.nn.softmax(rw, axis=-1)
        onehot = jax.nn.one_hot(sel, NUM_EXPERTS, dtype=rw.dtype)
        w = jnp.einsum('tk,tke->te', rw, onehot)
        h = jnp.einsum('td,erd->ter', xf, A)
        lora = jnp.einsum('ter,te,eor->to', h, w, B) * SCALING
        return (base + lora).reshape(bs, seq, -1)

    def _L1_xattn_ref(latents, context, Wq, Wk, Wv, Wo):
        import jax, jax.numpy as jnp
        import numpy as np
        import math
        HIDDEN = 512
        N_HEADS = 32
        HEAD_DIM = 128
        N_KV_HEADS = 4
        N_GROUPS = N_HEADS // N_KV_HEADS
        b, q_len, _ = latents.shape
        kv_len = q_len + context.shape[1]
        hidden_states = jnp.concatenate([context, latents], axis=1)
        q = (latents @ Wq).reshape(b, q_len, N_KV_HEADS, N_GROUPS, HEAD_DIM)
        k = (hidden_states @ Wk).reshape(b, kv_len, N_KV_HEADS, HEAD_DIM)
        v = (hidden_states @ Wv).reshape(b, kv_len, N_KV_HEADS, HEAD_DIM)
        scale = 1.0 / math.sqrt(HEAD_DIM)
        scores = jnp.einsum('bqhgd,bkhd->bhgqk', q, k) * scale
        attn = jax.nn.softmax(scores.astype(jnp.float32), axis=-1).astype(q.dtype)
        out = jnp.einsum('bhgqk,bkhd->bqhgd', attn, v)
        out = out.reshape(b, q_len, N_HEADS * HEAD_DIM)
        return out @ Wo

    def _L1_ffn_ref(x, W_base, b_base, W_gate, W_thr, b_thr, A, B):
        import jax, jax.numpy as jnp
        import numpy as np
        MAX_THRESHOLD = 1.0 / 8.0
        SCALING = 32.0 / 16.0
        base = jnp.einsum('bsd,od->bso', x, W_base) + b_base
        D = x.shape[-1]
        xf = x.reshape(-1, D)
        gate_logits = jax.nn.softmax(xf @ W_gate.T, axis=-1)
        thresholds = jax.nn.sigmoid(xf @ W_thr.T + b_thr) * MAX_THRESHOLD
        adapted = gate_logits - thresholds
        selected = (adapted >= 0).astype(x.dtype)
        weights = adapted * selected
        wsum = jnp.sum(weights, axis=-1, keepdims=True)
        wsum = jnp.where(wsum == 0, jnp.ones_like(wsum), wsum)
        weights = weights / wsum
        h = jnp.einsum('nd,erd->ner', xf, A)
        moe = jnp.einsum('ner,ne,eor->no', h, weights, B) * SCALING
        out = base + moe.reshape(base.shape)
        return out

    def _L2_xattn_ref(text, features, Wq, bq, Wk, bk):
        import jax, jax.numpy as jnp
        import numpy as np
        TEXT_DIM = 512
        FEATURE_DIM = 512

        def _xavier_uniform(key, shape):
            fan_in, fan_out = (shape[1], shape[0])
            limit = float(np.sqrt(6.0 / (fan_in + fan_out)))
            return jax.random.uniform(key, shape, jnp.float32, -limit, limit)
        Q = jnp.einsum('btx,dx->btd', text, Wq) + bq
        K = jnp.einsum('bpx,dx->bpd', features, Wk) + bk
        scale = 1.0 / jnp.sqrt(jnp.asarray(K.shape[-1], K.dtype))
        scores = jnp.einsum('btd,bpd->btp', Q, K) * scale
        attn = jax.nn.softmax(scores, axis=-1)
        attended = jnp.einsum('btp,bpd->btd', attn, features)
        return attended

    def _L2_ffn_ref(x, W, b):
        import jax, jax.numpy as jnp
        import numpy as np
        EPS = 1e-05

        def rms_norm(x):
            return x * jax.lax.rsqrt(jnp.mean(x * x, axis=-1, keepdims=True) + EPS)

        def activation_quant(x):
            scale = 127.0 / jnp.clip(jnp.max(jnp.abs(x), axis=-1, keepdims=True), EPS, None)
            return jnp.clip(jnp.round(x * scale), -128.0, 127.0) / scale

        def weight_quant(w):
            scale = 1.0 / jnp.clip(jnp.mean(jnp.abs(w)), EPS, None)
            return jnp.clip(jnp.round(w * scale), -1.0, 1.0) / scale
        xn = rms_norm(x)
        xq = xn + jax.lax.stop_gradient(activation_quant(xn) - xn)
        wq = W + jax.lax.stop_gradient(weight_quant(W) - W)
        y = jnp.einsum('bsd,od->bso', xq, wq) + b
        return x + jax.nn.gelu(y, approximate=False)

    def _L3_xattn_ref(hidden_states, cross_attention_states, attention_mask, Wq, Wk, Wv, Wo, q_norm_w, k_norm_w):
        import jax, jax.numpy as jnp
        import numpy as np
        B, Q, K, D = (1, 128, 6404, 512)
        H, KVH, HD = (32, 8, 128)
        GROUPS = H // KVH
        EPS = 1e-05

        def _rmsnorm(x, w):
            xf = x.astype(jnp.float32)
            var = jnp.mean(xf * xf, axis=-1, keepdims=True)
            return (xf * jax.lax.rsqrt(var + EPS)).astype(x.dtype) * w
        bsz, q_len, _ = hidden_states.shape
        kv_len = cross_attention_states.shape[1]
        q = (hidden_states @ Wq.T).reshape(bsz, q_len, H, HD).transpose(0, 2, 1, 3)
        k = (cross_attention_states @ Wk.T).reshape(bsz, kv_len, KVH, HD).transpose(0, 2, 1, 3)
        v = (cross_attention_states @ Wv.T).reshape(bsz, kv_len, KVH, HD).transpose(0, 2, 1, 3)
        q = _rmsnorm(q, q_norm_w)
        k = jnp.repeat(k, GROUPS, axis=1)
        v = jnp.repeat(v, GROUPS, axis=1)
        k = _rmsnorm(k, k_norm_w)
        scale = 1.0 / np.sqrt(HD)
        scores = jnp.einsum('bhqd,bhkd->bhqk', q, k) * scale
        scores = scores + attention_mask[:, :, :, :kv_len]
        probs = jax.nn.softmax(scores.astype(jnp.float32), axis=-1).astype(q.dtype)
        out = jnp.einsum('bhqk,bhkd->bhqd', probs, v)
        out = out.transpose(0, 2, 1, 3).reshape(bsz, q_len, H * HD)
        return out @ Wo.T

    def _L3_ffn_ref(x, A, B, Wr, br):
        import jax, jax.numpy as jnp
        import numpy as np
        ALPHA = 32
        R = 16
        SCALING = ALPHA / R
        H = A.shape[0]
        router_logits = jnp.einsum('bsd,hd->bsh', x, Wr) + br
        scores = H * jax.nn.softmax(router_logits, axis=-1)
        low = jnp.einsum('bsd,hrd->bshr', x, A)
        out = jnp.einsum('bshr,hor,bsh->bso', low, B, scores)
        return SCALING * out
    x = x + jnp.tanh(g_xattn[0]) * _L0_xattn_ref(_layernorm(x, axis=-1), ctx_4096, L0_xattn_Wq, L0_xattn_bq, L0_xattn_Wk, L0_xattn_bk, L0_xattn_Wv, L0_xattn_bv, L0_xattn_Wo, L0_xattn_bo)
    x = x + jnp.tanh(g_ffn[0]) * _L0_ffn_ref(_layernorm(x, axis=-1), L0_ffn_W_base, L0_ffn_b_base, L0_ffn_W_router, L0_ffn_A, L0_ffn_B)
    x = x + jnp.tanh(g_xattn[1]) * _L1_xattn_ref(_layernorm(x, axis=-1), ctx_4096, L1_xattn_Wq, L1_xattn_Wk, L1_xattn_Wv, L1_xattn_Wo)
    x = x + jnp.tanh(g_ffn[1]) * _L1_ffn_ref(_layernorm(x, axis=-1), L1_ffn_W_base, L1_ffn_b_base, L1_ffn_W_gate, L1_ffn_W_thr, L1_ffn_b_thr, L1_ffn_A, L1_ffn_B)
    x = x + jnp.tanh(g_xattn[2]) * _L2_xattn_ref(_layernorm(x, axis=-1), ctx_4096, L2_xattn_Wq, L2_xattn_bq, L2_xattn_Wk, L2_xattn_bk)
    x = x + jnp.tanh(g_ffn[2]) * _L2_ffn_ref(_layernorm(x, axis=-1), L2_ffn_W, L2_ffn_b)
    x = x + jnp.tanh(g_xattn[3]) * _L3_xattn_ref(_layernorm(x, axis=-1), ctx_4096, mask_1x1xSxS2_ff0, L3_xattn_Wq, L3_xattn_Wk, L3_xattn_Wv, L3_xattn_Wo, L3_xattn_q_norm_w, L3_xattn_k_norm_w)
    x = x + jnp.tanh(g_ffn[3]) * _L3_ffn_ref(_layernorm(x, axis=-1), L3_ffn_A, L3_ffn_B, L3_ffn_Wr, L3_ffn_br)
    return x

_drawn_inputs = setup_inputs


def setup_inputs(seed=0):
    import zlib

    import numpy as np

    out = dict(_drawn_inputs(seed))
    spreads = {'L0_xattn_bq': (0.0, 0.8),
     'L0_xattn_bk': (0.0, 2.0),
     'L0_xattn_bv': (0.0, 0.8),
     'L0_xattn_bo': (0.0, 0.1),
     'L2_xattn_bq': (0.0, 0.779),
     'L2_xattn_bk': (0.0, 2.0),
     'L3_xattn_q_norm_w': (1.0, 0.6),
     'L3_xattn_k_norm_w': (1.0, 0.6),
     'L3_ffn_br': (0.0, 0.571)}
    factors = {'L0_xattn_Wq': 8.0,
     'L0_xattn_Wk': 8.0,
     'L0_xattn_Wv': 8.0,
     'L0_xattn_Wo': 4.319,
     'L1_ffn_b_base': 8.0,
     'L2_ffn_b': 6.87,
     'L0_ffn_b_base': 3.068}
    for name, (base, spread) in spreads.items():
        noise = np.random.default_rng([zlib.crc32(name.encode()), seed]).standard_normal(out[name].shape)
        drawn = base * np.exp(spread * noise) if base else spread * noise
        out[name] = jnp.asarray(drawn.astype(out[name].dtype))
    for name, factor in factors.items():
        out[name] = (out[name] * factor).astype(out[name].dtype)
    return out
```

```python
import math
from contextlib import ExitStack

import numpy as np

import concourse.bass as bass
from concourse import mybir

F32 = mybir.dt.float32
F32R = mybir.dt.float32r
BF16 = mybir.dt.bfloat16
ALU = mybir.AluOpType
ACT = mybir.ActivationFunctionType
AX_X = mybir.AxisListType.X

P = 128
B, S, D = 32, 64, 512
BG = 8
G = B // BG
TG = BG * S
NT = TG // P
NC = D // P
EPS = 1e-5
BIG = 3.0e38
MAGIC = 12582912.0
LORA_SCALE = 2.0
E8, R16 = 8, 16
HEADS0, HD0, WIN = 8, 8, 16
TB = 16
KW = 2 * TB
PADT = WIN // 2 + D + WIN // 2
HD = 128


def wait(eng, sem, value):
    if type(value) is int and value <= 0:
        return
    eng.wait_ge(sem, value)


class Own:

    def __init__(self, eng, sem, base=0):
        self.eng, self.sem, self.base, self.n = eng, sem, base, 0

    def __call__(self, ins):
        self.n += 1
        ins.then_inc(self.sem, 1)
        self.eng.wait_ge(self.sem, self.base + self.n)


def build(nc, a, out, stages=8, groups=G):
    with ExitStack() as top:
        def sb(name, shape, dt=F32, ctx=top):
            return ctx.enter_context(nc.sbuf_tensor(name, shape, dt))

        live = []

        def sem(name):
            if not live:
                live.append(ExitStack())
            s = live[0].enter_context(nc.semaphore(name))
            live.append(s)
            return s

        def end_phase():
            nums = sorted(s.num for s in live[1:])
            runs = []
            for n in nums:
                if runs and runs[-1][1] == n:
                    runs[-1][1] = n + 1
                else:
                    runs.append([n, n + 1])
            with nc.Block() as blk:
                @blk.gpsimd
                def _(pool):
                    for first, stop in runs:
                        nc.gpsimd.sem_clear(range(first, stop))
            live[0].close()
            live.clear()

        ps = top.enter_context(nc.psum_tensor("ps", [P, 8, 512], F32))
        x = sb("x", [P, NT, D])
        xn = sb("xn", [P, NT, D])
        cnat = sb("cnat", [P, NT, D])
        Hh = sb("Hh", [P, NC, BG, 2, S], F32R)
        Hl = sb("Hl", [P, NC, BG, 2, S], F32R)
        bst = sb("bst", [P, NT, 6])
        mv = sb("mv", [P, NT, 2])
        rstd = sb("rstd", [P, NT])
        nt = sb("nt", [P, 2, NT])
        ident = sb("ident", [P, P])
        ones = sb("ones", [P, P])
        zb = sb("zb", [P, 512], BF16)
        identb = sb("identb", [P, P], BF16)
        hmask = sb("hmask", [P, HEADS0])
        band = sb("band", [P, KW])
        omask = sb("omask", [P, S])
        osel = sb("osel", [P, TB])
        bmask = sb("bmask", [P, P])
        vrow = sb("vrow", [1, 8, P])
        gates = sb("gates", [P, 8])
        tg = sb("tg", [P, 8])
        wbd = {n: sb("bd_" + n, [P, P]) for n in ("q", "k", "v", "o")}
        b0 = {n: sb("b0_" + n, [P, 1]) for n in ("q", "k", "o")}
        bvrow = sb("bvrow", [1, P])
        bbase = {n: sb("bbase_" + n, [1, D]) for n in ("0", "1")}
        bthr = sb("bthr", [P, 1])
        nbthr = sb("nbthr", [P, 1])
        br3 = sb("br3", [P, E8])
        bq2 = sb("bq2", [P, NC])
        bk2 = sb("bk2", [P, NC])
        bf2 = sb("bf2", [P, D])
        tern = sb("tern", [P, NC, D], BF16)
        wmean = sb("wmean", [P, 1])
        wsc = sb("wsc", [P, 4])
        mask3 = sb("mask3", [P, S])
        nw3 = sb("nw3", [P, 2])
        qkw = sb("qkw", [P, 1])

        def f(ap):
            return ap.bitcast(F32)

        l_c = sem("l_c")
        c_v = sem("c_v")
        c_a = sem("c_a")
        c_p = sem("c_p")
        c_z = sem("c_z")
        with ExitStack() as ph:
            wt = sb("wt", [P, NC, D], ctx=ph)
            wab = sb("wab", [P, NC, D], ctx=ph)
            loads = []
            for t, n in ((ident, "c_ident"), (hmask, "c_hmask"), (band, "c_band"), (omask, "c_omask"),
                         (osel, "c_osel"), (bmask, "c_bmask")):
                loads.append((t[:], a[n]))
            loads.append((vrow[:].rearrange("a q p -> a (q p)"), a["c_vrow"]))
            loads.append((gates[:, 0:4], a["g_xattn"].unsqueeze(0).broadcast_to((P, 4))))
            loads.append((gates[:, 4:8], a["g_ffn"].unsqueeze(0).broadcast_to((P, 4))))
            for n in ("q", "k", "v", "o"):
                for b in range(2):
                    loads.append((("bd", n, b), a[f"L0_W{n}T"]))
            for b in range(2):
                for n in ("q", "k", "o"):
                    loads.append((b0[n][64 * b:64 * b + 64, :], a[f"L0_xattn_b{n}"].unsqueeze(1)))
                loads.append((bvrow[:, 64 * b:64 * b + 64], a["L0_xattn_bv"].unsqueeze(0)))
                loads.append((mask3[64 * b:64 * b + 64, :], a["mask"]))
            loads.append((bbase["0"][:], a["L0_ffn_b_base"].unsqueeze(0)))
            loads.append((bbase["1"][:], a["L1_ffn_b_base"].unsqueeze(0)))
            loads.append((bthr[:], a["L1_ffn_b_thr"].unsqueeze(0).broadcast_to((P, 1))))
            loads.append((br3[:], a["L3_ffn_br"].unsqueeze(0).broadcast_to((P, E8))))
            loads.append((bq2[:], a["L2_bq"]))
            loads.append((bk2[:], a["L2_bk"]))
            loads.append((bf2[:], a["L2_ffn_b"].unsqueeze(0).broadcast_to((P, D))))
            loads.append((nw3[:, 0:1], a["L3_xattn_q_norm_w"].unsqueeze(1)))
            loads.append((nw3[:, 1:2], a["L3_xattn_k_norm_w"].unsqueeze(1)))
            loads.append((wt[:], a["L2_ffn_WT"]))
            with nc.Block() as blk:
                @blk.sync
                def _(sp):
                    sp.wait_ge(c_z, 4)
                    for dst, src in loads:
                        if type(dst) is tuple:
                            _, n, b = dst
                            dst = wbd[n][64 * b:64 * b + 64, 64 * b:64 * b + 64]
                        sp.dma_start(dst, src).then_inc(l_c, 16)

                @blk.gpsimd
                def _(pool):
                    for n in ("q", "k", "v", "o"):
                        nc.gpsimd.memset(wbd[n][:], 0.0).then_inc(c_z, 1)
                    nc.gpsimd.memset(ones[:], 1.0).then_inc(c_p, 1)
                    nc.gpsimd.memset(zb[:], 0.0).then_inc(c_p, 1)

                @blk.scalar
                def _(act):
                    act.wait_ge(l_c, 16 * len(loads))
                    nc.scalar.activation(tg[:], gates[:], ACT.Tanh).then_inc(c_a, 1)
                    nc.scalar.activation(wab[:], wt[:], ACT.Abs, accum_out=wmean[:]).then_inc(c_a, 1)

                @blk.tensor
                def _(pe):
                    pe.wait_ge(c_p, 2)
                    pe.wait_ge(c_a, 2)
                    nc.tensor.matmul(ps[:, 0, 0:1], ones[:], wmean[:], start=True, stop=True).then_inc(c_p, 1)

                @blk.vector
                def _(dve):
                    own = Own(dve, c_v)
                    dve.wait_ge(l_c, 16 * len(loads))
                    own(nc.vector.tensor_copy(identb[:], ident[:]))
                    own(nc.vector.tensor_scalar(nbthr[:], bthr[:], -1.0, None, ALU.mult))
                    own(nc.vector.tensor_tensor(qkw[:], nw3[:, 0:1], nw3[:, 1:2], ALU.mult))
                    dve.wait_ge(c_p, 3)
                    own(nc.vector.tensor_scalar(wsc[:, 0:1], ps[:, 0, 0:1], 1.0 / (D * D), EPS, ALU.mult, ALU.max))
                    own(nc.vector.reciprocal(wsc[:, 1:2], wsc[:, 0:1]))
                    own(nc.vector.tensor_scalar(wab[:], wt[:], wsc[:, 1:2], None, ALU.mult))
                    own(nc.vector.tensor_scalar(wab[:], wab[:], MAGIC, None, ALU.add))
                    own(nc.vector.tensor_scalar(wab[:], wab[:], MAGIC, -1.0, ALU.subtract, ALU.max))
                    own(nc.vector.tensor_scalar(tern[:], wab[:], 1.0, None, ALU.min))

        def root(act, dst, src, own, done, scale=1.0, bias=0.0, factor=0.0):
            nc.scalar.activation(dst, src, ACT.Ln, scale=scale, bias=bias).then_inc(own, 1)
            act.wait_ge(own, done + 1)
            nc.scalar.activation(dst, dst, ACT.Exp, scale=-0.5, bias=factor).then_inc(own, 1)

        def newton(own, y, v, t):
            own(nc.vector.tensor_tensor(t, y, y, ALU.mult))
            own(nc.vector.tensor_tensor(t, t, v, ALU.mult))
            own(nc.vector.tensor_scalar(t, t, -0.5, 1.5, ALU.mult, ALU.add))
            own(nc.vector.tensor_tensor(y, y, t, ALU.mult))

        def layer_norm(tag, flat=None):
            v_own, v_xn, s_xt, a_xh, v_xl, a_rs = (
                sem(f"{n}_{tag}") for n in ("v_lnown", "v_xn", "s_xt", "a_xh", "v_xl", "a_rs"))

            def dve_rows(dve):
                own = Own(dve, v_own)
                for j in range(NT):
                    last = nc.vector.bn_stats(bst[:, j, :], x[:, j, :])
                own(last)
                for j in range(NT):
                    last = nc.vector.bn_aggr(mv[:, j, :], bst[:, j, :])
                own(last)
                own(nc.vector.tensor_scalar(nt[:, 0], mv[:, :, 1], EPS, None, ALU.add))
                dve.wait_ge(a_rs, 2)
                newton(own, rstd[:], nt[:, 0], nt[:, 1])
                for j in range(NT):
                    nc.vector.tensor_scalar(xn[:, j, :], x[:, j, :], mv[:, j, 0:1], rstd[:, j:j + 1],
                                            ALU.subtract, ALU.mult).then_inc(v_xn, 1)

            def act_root(act):
                act.wait_ge(v_own, 3)
                root(act, rstd[:], nt[:, 0], a_rs, 0)

            def pe_turn(pe):
                for j in range(NT):
                    pe.wait_ge(v_xn, j + 1)
                    for c in range(NC):
                        last = nc.tensor.transpose(ps[:, j, c * P:(c + 1) * P], xn[:, j, c * P:(c + 1) * P], ident[:])
                    last.then_inc(s_xt, 1)

            def place(part, j):
                if flat:
                    return flat[part][:, :, j * P:(j + 1) * P]
                return (Hh, Hl)[part][:, :, 2 * j:2 * j + 2, 1, :]

            def cols(j):
                if flat:
                    return ps[:, j, :].rearrange("p (c t) -> p c t", c=NC)
                return ps[:, j, :].rearrange("p (c b t) -> p c b t", c=NC, b=2)

            def act_high(act):
                for j in range(NT):
                    act.wait_ge(s_xt, j + 1)
                    nc.scalar.copy(place(0, j), cols(j)).then_inc(a_xh, 1)

            def dve_low(dve):
                for j in range(NT):
                    dve.wait_ge(a_xh, j + 1)
                    nc.vector.tensor_tensor(place(1, j), cols(j), f(place(0, j)), ALU.subtract).then_inc(v_xl, 1)

            return dve_rows, pe_turn, act_high, dve_low, v_xn, v_xl, act_root

        def passes(pe, dst, lh, ll, rh, rl, start, stop, **kw):
            nc.tensor.matmul(dst, lh, rh, start=start, stop=False, **kw)
            nc.tensor.matmul(dst, lh, rl, start=False, stop=False, **kw)
            return nc.tensor.matmul(dst, ll, rh, start=False, stop=stop, **kw)

        def phase_load(g):
            l_x, a_ch, v_cl = sem("l_x"), sem("a_ch"), sem("v_cl")
            with ExitStack() as ph:
                craw = sb("craw", [P, NC, BG, S], ctx=ph)
                with nc.Block() as blk:
                    @blk.sync
                    def _(sp):
                        one = lambda n: a[n][bass.ds(g, 1)].rearrange("a p t d -> (a p) t d")
                        sp.dma_start(x[:], one("x")).then_inc(l_x, 16)
                        sp.dma_start(cnat[:], one("ctx")).then_inc(l_x, 16)
                        sp.dma_start(craw[:].rearrange("p c b t -> p c (b t)"), one("ctxT")).then_inc(l_x, 16)

                    @blk.scalar
                    def _(act):
                        act.wait_ge(l_x, 48)
                        for c in range(NC):
                            nc.scalar.copy(Hh[:, c, :, 0, :], craw[:, c]).then_inc(a_ch, 1)

                    @blk.vector
                    def _(dve):
                        for c in range(NC):
                            dve.wait_ge(a_ch, c + 1)
                            nc.vector.tensor_tensor(Hl[:, c, :, 0, :], craw[:, c], f(Hh[:, c, :, 0, :]),
                                                    ALU.subtract).then_inc(v_cl, 1)

        def phase_local():
            dve_rows, _, _, _, v_xn, _, act_root = layer_norm("l0")
            p_z, a_cp, s_p, a_p, v_qx, a_vx = (sem(n) for n in ("p_z", "a_cp", "s_p", "a_p", "v_qx", "a_vx"))
            s_s, v_s, v_sub, a_e, v_pr, s_t, a_t, s_av, v_om, s_sel, a_o, s_wo, v_x = (
                sem("o_" + n) for n in ("s_s", "v_s", "v_sub", "a_e", "v_pr", "s_t", "a_t", "s_av", "v_om", "s_sel",
                                        "a_o", "s_wo", "v_x"))
            v_own = sem("o_own")
            NQ = 4
            NB = D // TB // NQ
            SC = float(HD0) ** -0.5
            with ExitStack() as ph:
                qx = sb("qx", [P, D // TB, HEADS0, TB], ctx=ph)
                qs = sb("qs", [P, D], ctx=ph)
                kp = sb("kp", [P, PADT], ctx=ph)
                cp = sb("cp", [P, PADT], ctx=ph)
                cw = sb("cw", [P, D // TB, KW], ctx=ph)
                vx = sb("vx", [P, 8, 2, 4, S], ctx=ph)
                sc = sb("sc", [P, 2, NB, KW], ctx=ph)
                ex = sb("ex", [P, 2, NB, KW], ctx=ph)
                pr = sb("pr", [P, 2, NB, KW], ctx=ph)
                st = sb("st", [P, 3, 2, NB], ctx=ph)
                at = sb("at", [P, 4, P], ctx=ph)
                om = sb("om", [P, NB, 2, S], ctx=ph)
                oc = sb("oc", [P, D], ctx=ph)
                tmp = sb("tmp", [P, D], ctx=ph)
                SB_, TBK, AB, CB, PB = 0, 2, 3, 5, 6
                sv = ps[:, SB_:SB_ + 2, 0:NB * KW].rearrange("p b (n k) -> p b n k", n=NB)
                with nc.Block() as blk:
                    @blk.gpsimd
                    def _(pool):
                        nc.gpsimd.memset(vx[:], 0.0).then_inc(p_z, 1)
                        nc.gpsimd.memset(kp[:], 0.0).then_inc(p_z, 1)
                        nc.gpsimd.memset(cp[:], 0.0).then_inc(p_z, 1)

                    @blk.tensor
                    def _(pe):
                        pe.wait_ge(v_xn, NT)
                        with pe.Fori(0, NT) as j:
                            pe.wait_ge(v_x, j)
                            nc.tensor.matmul(ps[:, PB, :], wbd["q"][:],
                                             xn[:, bass.ds(j, 1), :].rearrange("p a d -> p (a d)"),
                                             start=True, stop=True).then_inc(s_p, 1)
                            pe.wait_ge(a_cp, 2 * j + 2)
                            nc.tensor.matmul(ps[:, PB + 1, :], wbd["k"][:], cp[:, WIN // 2:WIN // 2 + D],
                                             start=True, stop=True).then_inc(s_p, 1)
                            for q in range(8):
                                keys = cw[:, 4 * q:4 * q + 4, :].rearrange("p n k -> p (n k)")
                                dst = ps[:, AB + q // 4, (q % 4) * P:(q % 4 + 1) * P]
                                nc.tensor.matmul(dst, keys, wbd["v"][:], start=True, stop=False)
                                last = nc.tensor.matmul(dst, vrow[:, q, :], bvrow[:], start=False, stop=True)
                            last.then_inc(s_p, 1)

                            def turn(n):
                                pe.wait_ge(v_pr, NQ * j + n + 1)
                                if n == 0:
                                    pe.wait_ge(a_t, NQ * j)
                                else:
                                    pe.wait_ge(a_t, NQ * j + n)
                                for b in range(2):
                                    for q in range(2):
                                        last = nc.tensor.transpose(
                                            ps[:, TBK, (2 * b + q) * P:(2 * b + q + 1) * P],
                                            pr[:, b, 4 * q:4 * q + 4, :].rearrange("p n k -> p (n k)"), ident[:])
                                last.then_inc(s_t, 1)

                            def values(n):
                                pe.wait_ge(a_t, NQ * j + n + 1)
                                if n == 0:
                                    pe.wait_ge(a_vx, j + 1)
                                else:
                                    pe.wait_ge(v_om, NQ * j + n)
                                for b in range(2):
                                    for q in range(2):
                                        last = nc.tensor.matmul(
                                            ps[:, AB + b, q * 256:(q + 1) * 256], at[:, 2 * b + q, :],
                                            vx[:, 2 * n + q, b].rearrange("p n o -> p (n o)"), start=True, stop=True)
                                last.then_inc(s_av, 1)

                            def pick(n):
                                pe.wait_ge(v_om, NQ * j + n + 1)
                                for t in range(NB):
                                    col = (n * NB + t) * TB
                                    last = nc.tensor.matmul(ps[:, CB, col:col + TB],
                                                            om[:, t].rearrange("p b o -> p (b o)"), osel[:],
                                                            start=True, stop=True)
                                last.then_inc(s_sel, 1)

                            for n in range(NQ + 2):
                                if n < NQ:
                                    if n == 0:
                                        pe.wait_ge(v_qx, j + 1)
                                        pe.wait_ge(a_p, 2 * j + 2)
                                    else:
                                        pe.wait_ge(v_s, NQ * j + n)
                                    for b in range(2):
                                        for t in range(NB):
                                            t0 = (n * NB + t) * TB
                                            last = nc.tensor.matmul(
                                                ps[:, SB_ + b, t * KW:(t + 1) * KW],
                                                qx[64 * b:64 * b + 64, n * NB + t].rearrange("p h t -> p (h t)"), kp[64 * b:64 * b + 64, t0:t0 + KW],
                                                start=True, stop=True)
                                    last.then_inc(s_s, 1)
                                if 1 <= n <= NQ:
                                    turn(n - 1)
                                if n >= 2:
                                    pick(n - 2)
                                if 1 <= n <= NQ:
                                    values(n - 1)
                            pe.wait_ge(a_o, j + 1)
                            nc.tensor.matmul(ps[:, PB, :], wbd["o"][:], oc[:], start=True, stop=True).then_inc(s_wo, 1)

                    @blk.scalar
                    def _(act):
                        act_root(act)
                        act.wait_ge(p_z, 3)
                        with act.Fori(0, NT) as j:
                            wait(act, s_p, 3 * j)
                            nc.scalar.copy(cp[:, WIN // 2:WIN // 2 + D],
                                           cnat[:, bass.ds(j, 1), :].rearrange("p a d -> p (a d)")).then_inc(a_cp, 1)
                            act.wait_ge(a_cp, 2 * j + 1)
                            nc.scalar.copy(cw[:], bass.AP(cp[:].tensor, 0, [[PADT, P], [TB, D // TB], [1, KW]])).then_inc(a_cp, 1)
                            act.wait_ge(s_p, 3 * j + 1)
                            nc.scalar.activation(qs[:], ps[:, PB, :], ACT.Identity, bias=b0["q"][:]).then_inc(a_p, 1)
                            act.wait_ge(s_p, 3 * j + 2)
                            nc.scalar.activation(kp[:, WIN // 2:WIN // 2 + D], ps[:, PB + 1, :], ACT.Identity,
                                                 bias=b0["k"][:]).then_inc(a_p, 1)
                            act.wait_ge(s_p, 3 * j + 3)
                            for t in range(4):
                                r = slice(32 * t, 32 * t + 32)
                                last = nc.scalar.copy(
                                    vx[r, :, :, t, :],
                                    ps[r, AB:AB + 2, :].rearrange("p a (q b o) -> p (a q) b o", q=4, b=2))
                            last.then_inc(a_vx, 1)
                            for n in range(NQ + 1):
                                if n < NQ:
                                    act.wait_ge(v_sub, NQ * j + n + 1)
                                    nc.scalar.activation(ex[:], sc[:], ACT.Exp, scale=SC).then_inc(a_e, 1)
                                if n >= 1:
                                    act.wait_ge(s_t, NQ * j + n)
                                    nc.scalar.copy(at[:], ps[:, TBK, :].rearrange("p (n k) -> p n k", n=4)).then_inc(a_t, 1)
                            act.wait_ge(s_sel, NQ * (j + 1))
                            nc.scalar.copy(oc[:], ps[:, CB, :]).then_inc(a_o, 1)

                    @blk.vector
                    def _(dve):
                        dve_rows(dve)
                        per_tile = 2 + NQ * 3
                        with dve.Fori(0, NT) as j:
                            own = Own(dve, v_own, per_tile * j)
                            dve.wait_ge(a_p, 2 * j + 1)
                            for h in range(HEADS0):
                                last = nc.vector.tensor_scalar(qx[:, :, h, :], qs[:].rearrange("p (n t) -> p n t", t=TB), hmask[:, h:h + 1], None, ALU.mult)
                            last.then_inc(v_qx, 1)

                            def masked(n):
                                dve.wait_ge(s_av, NQ * j + n + 1)
                                if n > 0:
                                    dve.wait_ge(s_sel, NQ * j + n)
                                nc.vector.tensor_tensor(
                                    om[:].rearrange("p n b o -> p b n o"),
                                    ps[:, AB:AB + 2, :].rearrange("p b (n o) -> p b n o", n=NB),
                                    omask[:].unsqueeze(1).unsqueeze(1).broadcast_to((P, 2, NB, S)),
                                    ALU.mult).then_inc(v_om, 1)

                            for n in range(NQ):
                                dve.wait_ge(s_s, NQ * j + n + 1)
                                bc = lambda y: y.unsqueeze(3).broadcast_to((P, 2, NB, KW))
                                own(nc.vector.tensor_tensor(sc[:], sv, band[:].unsqueeze(1).unsqueeze(1).broadcast_to(
                                    (P, 2, NB, KW)), ALU.add))
                                nc.vector.tensor_reduce(st[:, 0], sc[:], AX_X, ALU.max).then_inc(v_s, 1)
                                dve.wait_ge(v_s, NQ * j + n + 1)
                                nc.vector.tensor_tensor(sc[:], sc[:], bc(st[:, 0]), ALU.subtract).then_inc(v_sub, 1)
                                if n > 0:
                                    masked(n - 1)
                                dve.wait_ge(a_e, NQ * j + n + 1)
                                own(nc.vector.tensor_reduce(st[:, 1], ex[:], AX_X, ALU.add))
                                own(nc.vector.reciprocal(st[:, 2], st[:, 1]))
                                if n > 0:
                                    dve.wait_ge(s_t, NQ * j + n)
                                nc.vector.tensor_tensor(pr[:], ex[:], bc(st[:, 2]), ALU.mult).then_inc(v_pr, 1)
                            masked(NQ - 1)
                            dve.wait_ge(s_wo, j + 1)
                            xj = x[:, bass.ds(j, 1), :].rearrange("p a d -> p (a d)")
                            own(nc.vector.tensor_scalar(tmp[:], ps[:, PB, :], b0["o"][:], tg[:, 0:1], ALU.add, ALU.mult))
                            own(nc.vector.tensor_tensor(xj, xj, tmp[:], ALU.add))
                            assert own.n == per_tile, own.n
                            nc.vector.tensor_copy(st[:, 0, 0, 0:1], st[:, 1, 0, 0:1]).then_inc(v_x, 1)

        def phase_mixture(tag, gate, n_base, n_gate, wcat, wb, bias):
            l_w, a_w, p_w, s_ag, v_h, s_ht, a_ht, v_ht, s_y, v_own, v_z, a_z = (
                sem(f"m{tag}_{n}") for n in ("l_w", "a_w", "p_w", "s_ag", "v_h", "s_ht", "a_ht", "v_ht", "s_y", "own",
                                             "v_z", "a_z"))
            NW = n_base + P + n_gate
            RB = E8 * R16
            with ExitStack() as ph:
                xh = sb("mxh" + tag, [P, NC, TG], F32R, ctx=ph)
                xl = sb("mxl" + tag, [P, NC, TG], F32R, ctx=ph)
                dve_rows, pe_turn, act_high, dve_low, v_xn, v_xl, act_root = layer_norm("m" + tag, (xh, xl))
                wr = sb("mwr" + tag, [P, NC, NW], ctx=ph)
                wh = sb("mwh" + tag, [P, NC, NW], F32R, ctx=ph)
                wl = sb("mwl" + tag, [P, NC, NW], F32R, ctx=ph)
                br = sb("mbr" + tag, [P, D], ctx=ph)
                bh = sb("mbh" + tag, [P, D], F32R, ctx=ph)
                bl = sb("mbl" + tag, [P, D], F32R, ctx=ph)
                z = sb("mz" + tag, [P, NT, 16], ctx=ph)
                z2 = sb("mz2" + tag, [P, NT, 16], ctx=ph)
                m8 = sb("mm8" + tag, [P, NT, 8], ctx=ph)
                e = sb("me" + tag, [P, NT, E8], ctx=ph)
                w = sb("mw" + tag, [P, NT, E8], ctx=ph)
                s1 = sb("ms1" + tag, [P, 6, NT], ctx=ph)
                hp = sb("mhp" + tag, [P, NT, E8, R16], ctx=ph)
                th = sb("mth" + tag, [P, NT, P], F32R, ctx=ph)
                tl = sb("mtl" + tag, [P, NT, P], F32R, ctx=ph)
                with nc.Block() as blk:
                    @blk.sync
                    def _(sp):
                        sp.dma_start(wr[:], wcat).then_inc(l_w, 16)
                        sp.dma_start(br[:], wb).then_inc(l_w, 16)

                    @blk.gpsimd
                    def _(pool):
                        for c in range(NC):
                            pool.wait_ge(a_w, c + 1)
                            nc.gpsimd.tensor_tensor(wl[:, c], wr[:, c], f(wh[:, c]), ALU.subtract).then_inc(p_w, 1)
                        pool.wait_ge(a_w, NC + 1)
                        nc.gpsimd.tensor_tensor(bl[:], br[:], f(bh[:]), ALU.subtract).then_inc(p_w, 1)

                    @blk.scalar
                    def _(act):
                        act_root(act)
                        act.wait_ge(l_w, 32)
                        for c in range(NC):
                            nc.scalar.copy(wh[:, c], wr[:, c]).then_inc(a_w, 1)
                        nc.scalar.copy(bh[:], br[:]).then_inc(a_w, 1)
                        act_high(act)
                        if gate == "threshold":
                            act.wait_ge(v_z, 1)
                            nc.scalar.activation(s1[:, 2, :], z[:, :, E8], ACT.Exp, bias=nbthr[:], scale=-1.0)
                        act.wait_ge(v_z, 1)
                        nc.scalar.activation(e[:], z2[:, :, 0:E8], ACT.Exp).then_inc(a_z, 1)
                        for j in range(NT):
                            act.wait_ge(s_ht, j + 1)
                            nc.scalar.copy(th[:, j, :], ps[:, j, 256:384]).then_inc(a_ht, 1)

                    @blk.tensor
                    def _(pe):
                        pe_turn(pe)
                        for j in range(NT):
                            pe.wait_ge(v_xl, j + 1)
                            rows = slice(j * P, (j + 1) * P)
                            for c in range(NC):
                                if j == 0:
                                    pe.wait_ge(p_w, c + 1)
                                last = passes(pe, ps[:, j, 0:P + n_gate], xh[:, c, rows], xl[:, c, rows],
                                              wh[:, c, n_base:NW], wl[:, c, n_base:NW], c == 0, c == NC - 1)
                            last.then_inc(s_ag, 1)
                            if n_base:
                                nc.tensor.matmul(ps[:, 4 + j, :], ones[0:1, :], bias[:], start=True, stop=False)
                                for c in range(NC):
                                    passes(pe, ps[:, 4 + j, :], xh[:, c, rows], xl[:, c, rows],
                                           wh[:, c, 0:n_base], wl[:, c, 0:n_base], False, False)
                        pe.wait_ge(p_w, NC + 1)
                        for j in range(NT):
                            pe.wait_ge(v_h, j + 1)
                            nc.tensor.transpose(ps[:, j, 256:384], hp[:, j].rearrange("p e r -> p (e r)"),
                                                ident[:]).then_inc(s_ht, 1)
                            if j > 0:
                                pe.wait_ge(v_ht, j)
                                passes(pe, ps[:, 3 + j, :], th[:, j - 1, :], tl[:, j - 1, :], bh[:], bl[:], not n_base,
                                       True).then_inc(s_y, 1)
                        pe.wait_ge(v_ht, NT)
                        passes(pe, ps[:, 3 + NT, :], th[:, NT - 1, :], tl[:, NT - 1, :], bh[:], bl[:], not n_base,
                               True).then_inc(s_y, 1)

                    @blk.vector
                    def _(dve):
                        dve_rows(dve)
                        dve_low(dve)
                        own = Own(dve, v_own)
                        bc = lambda y: y.unsqueeze(2).broadcast_to((P, NT, E8))
                        logit = z[:, :, 0:E8]
                        dve.wait_ge(s_ag, NT)
                        own(nc.vector.memset(z[:], -BIG))
                        own(nc.vector.tensor_copy(z[:, :, 0:n_gate], ps[:, 0:NT, P:P + n_gate]))
                        if gate == "softmax":
                            own(nc.vector.tensor_tensor(logit, logit, br3[:].unsqueeze(1).broadcast_to((P, NT, E8)),
                                                        ALU.add))
                        own(nc.vector.tensor_reduce(s1[:, 0, :], logit, AX_X, ALU.max))
                        nc.vector.tensor_tensor(z2[:, :, 0:E8], logit, bc(s1[:, 0, :]), ALU.subtract).then_inc(v_z, 1)
                        if gate == "top2":
                            own(nc.vector.memset(m8[:], -BIG))
                            for j in range(NT):
                                own(nc.vector.max(w[:, j, :], z[:, j, 0:E8]))
                            own(nc.vector.tensor_copy(m8[:, :, 0:2], w[:, :, 0:2]))
                            dve.wait_ge(a_z, 1)
                            for j in range(NT):
                                own(nc.vector.match_replace(z2[:, j, :], m8[:, j, :], z[:, j, :], BIG))
                            own(nc.vector.tensor_tensor(w[:], z2[:, :, 0:E8], logit, ALU.not_equal))
                            own(nc.vector.tensor_tensor(e[:], e[:], w[:], ALU.mult))
                        dve.wait_ge(a_z, 1)
                        own(nc.vector.tensor_reduce(s1[:, 1, :], e[:], AX_X, ALU.add))
                        own(nc.vector.reciprocal(s1[:, 1, :], s1[:, 1, :]))
                        own(nc.vector.tensor_tensor(w[:], e[:], bc(s1[:, 1, :]), ALU.mult))
                        scale = LORA_SCALE
                        if gate == "threshold":
                            own(nc.vector.tensor_scalar(s1[:, 2, :], s1[:, 2, :], 1.0, None, ALU.add))
                            own(nc.vector.reciprocal(s1[:, 2, :], s1[:, 2, :]))
                            own(nc.vector.tensor_scalar(s1[:, 2, :], s1[:, 2, :], 1.0 / 8.0, None, ALU.mult))
                            own(nc.vector.tensor_tensor(w[:], w[:], bc(s1[:, 2, :]), ALU.subtract))
                            own(nc.vector.tensor_scalar(w[:], w[:], 0.0, None, ALU.max))
                            own(nc.vector.tensor_reduce(s1[:, 3, :], w[:], AX_X, ALU.add))
                            own(nc.vector.tensor_scalar(s1[:, 4, :], s1[:, 3, :], 0.0, None, ALU.is_equal))
                            own(nc.vector.tensor_tensor(s1[:, 3, :], s1[:, 3, :], s1[:, 4, :], ALU.add))
                            own(nc.vector.reciprocal(s1[:, 3, :], s1[:, 3, :]))
                            own(nc.vector.tensor_tensor(w[:], w[:], bc(s1[:, 3, :]), ALU.mult))
                        if gate == "softmax":
                            scale = LORA_SCALE * E8
                        own(nc.vector.tensor_scalar(w[:], w[:], scale, None, ALU.mult))
                        for j in range(NT):
                            nc.vector.tensor_tensor(hp[:, j], ps[:, j, 0:RB].rearrange("p (e r) -> p e r", e=E8),
                                                    w[:, j, :].unsqueeze(2).broadcast_to((P, E8, R16)),
                                                    ALU.mult).then_inc(v_h, 1)
                        for j in range(NT):
                            dve.wait_ge(a_ht, j + 1)
                            nc.vector.tensor_tensor(tl[:, j, :], ps[:, j, 256:384], f(th[:, j, :]),
                                                    ALU.subtract).then_inc(v_ht, 1)
                        for j in range(NT):
                            dve.wait_ge(s_y, j + 1)
                            nc.vector.scalar_tensor_tensor(out=x[:, j, :], in0=ps[:, 4 + j, :],
                                                           scalar=tg[:, 4 + int(tag):5 + int(tag)], in1=x[:, j, :],
                                                           op0=ALU.mult, op1=ALU.add)

        def phase_text():
            dve_rows, pe_turn, act_high, dve_low, v_xn, v_xl, act_root = layer_norm("t")
            l_w, a_w, p_w, s_p, a_p, v_p, s_s, v_m, a_e, v_pr, s_t, a_t, v_t, s_y, v_own, a_c, p_c = (
                sem("t_" + n) for n in ("l_w", "a_w", "p_w", "s_p", "a_p", "v_p", "s_s", "v_m", "a_e", "v_pr", "s_t",
                                        "a_t", "v_t", "s_y", "own", "a_c", "p_c"))
            SCALE = float(D) ** -0.5
            with ExitStack() as ph:
                wr = sb("twr", [P, 2, NC, D], ctx=ph)
                wh = sb("twh", [P, 2, NC, D], F32R, ctx=ph)
                wl = sb("twl", [P, 2, NC, D], F32R, ctx=ph)
                qh = sb("tqh", [P, 2, NC, TG], F32R, ctx=ph)
                ql = sb("tql", [P, 2, NC, TG], F32R, ctx=ph)
                cnh = sb("tch", [P, NT, D], F32R, ctx=ph)
                cnl = sb("tcl", [P, NT, D], F32R, ctx=ph)
                sc = sb("tsc", [P, NT, P], ctx=ph)
                ex = sb("tex", [P, NT, P], ctx=ph)
                st = sb("tst", [P, 3, NT], ctx=ph)
                th = sb("tth", [P, NT, P], F32R, ctx=ph)
                tl = sb("ttl", [P, NT, P], F32R, ctx=ph)
                bias = (bq2, bk2)
                with nc.Block() as blk:
                    @blk.sync
                    def _(sp):
                        sp.dma_start(wr[:, 1], a["L2_WkT"]).then_inc(l_w, 16)
                        sp.wait_ge(l_w, 16)
                        sp.dma_start(wr[:, 0], a["L2_WqT"]).then_inc(l_w, 16)

                    @blk.gpsimd
                    def _(pool):
                        for n, m in enumerate((1, 0)):
                            for c in range(NC):
                                pool.wait_ge(a_w, NC * n + c + 1)
                                nc.gpsimd.tensor_tensor(wl[:, m, c], wr[:, m, c], f(wh[:, m, c]),
                                                        ALU.subtract).then_inc(p_w, 1)
                        for j in range(NT):
                            pool.wait_ge(a_c, j + 1)
                            nc.gpsimd.tensor_tensor(cnl[:, j], cnat[:, j], f(cnh[:, j]), ALU.subtract).then_inc(p_c, 1)

                    @blk.scalar
                    def _(act):
                        act_root(act)
                        for n, m in enumerate((1, 0)):
                            act.wait_ge(l_w, 16 * (n + 1))
                            for c in range(NC):
                                nc.scalar.copy(wh[:, m, c], wr[:, m, c]).then_inc(a_w, 1)
                        act_high(act)
                        for n, m in enumerate((1, 0)):
                            for c in range(NC):
                                act.wait_ge(s_p, NC * n + c + 1)
                                nc.scalar.activation(qh[:, m, c], ps[:, 4 + c, :], ACT.Identity,
                                                     bias=bias[m][:, c:c + 1]).then_inc(a_p, 1)
                        for j in range(NT):
                            nc.scalar.copy(cnh[:, j], cnat[:, j]).then_inc(a_c, 1)
                        act.wait_ge(v_m, 1)
                        nc.scalar.activation(ex[:], sc[:], ACT.Exp, scale=SCALE).then_inc(a_e, 1)
                        act.wait_ge(s_t, 1)
                        nc.scalar.copy(th[:], ps[:, 1, :].rearrange("p (j k) -> p j k", j=NT)).then_inc(a_t, 1)

                    @blk.tensor
                    def _(pe):
                        def project(n, m):
                            for e in range(NC):
                                if n:
                                    pe.wait_ge(v_p, e + 1)
                                for c in range(NC):
                                    pe.wait_ge(p_w, NC * n + c + 1)
                                    last = passes(pe, ps[:, 4 + e, :], wh[:, m, c, e * P:(e + 1) * P],
                                                  wl[:, m, c, e * P:(e + 1) * P], Hh[:, c, :, 1 - m, :],
                                                  Hl[:, c, :, 1 - m, :], c == 0, c == NC - 1)
                                last.then_inc(s_p, 1)
                        project(0, 1)
                        pe_turn(pe)
                        pe.wait_ge(v_xl, NT)
                        project(1, 0)
                        pe.wait_ge(v_p, 2 * NC)
                        for j in range(NT):
                            cols = slice(j * P, (j + 1) * P)
                            for c in range(NC):
                                last = passes(pe, ps[:, 0, cols], qh[:, 0, c, cols], ql[:, 0, c, cols],
                                              qh[:, 1, c, cols], ql[:, 1, c, cols], c == 0, c == NC - 1)
                        last.then_inc(s_s, 1)
                        pe.wait_ge(v_pr, 1)
                        for j in range(NT):
                            last = nc.tensor.transpose(ps[:, 1, j * P:(j + 1) * P], ex[:, j, :], ident[:])
                        last.then_inc(s_t, 1)
                        pe.wait_ge(v_t, 1)
                        pe.wait_ge(p_c, NT)
                        for j in range(NT):
                            passes(pe, ps[:, 4 + j, :], th[:, j, :], tl[:, j, :], cnh[:, j], cnl[:, j], True,
                                   True).then_inc(s_y, 1)

                    @blk.vector
                    def _(dve):
                        def low(n, m):
                            for e in range(NC):
                                dve.wait_ge(a_p, NC * n + e + 1)
                                nc.vector.scalar_tensor_tensor(out=ql[:, m, e], in0=ps[:, 4 + e, :],
                                                               scalar=bias[m][:, e:e + 1], in1=f(qh[:, m, e]),
                                                               op0=ALU.add, op1=ALU.subtract).then_inc(v_p, 1)
                        dve_rows(dve)
                        dve_low(dve)
                        low(0, 1)
                        low(1, 0)
                        own = Own(dve, v_own)
                        bc = lambda y: y.unsqueeze(2).broadcast_to((P, NT, P))
                        dve.wait_ge(s_s, 1)
                        own(nc.vector.tensor_tensor(sc[:], ps[:, 0, :].rearrange("p (j k) -> p j k", j=NT),
                                                    bmask[:].unsqueeze(1).broadcast_to((P, NT, P)), ALU.add))
                        own(nc.vector.tensor_reduce(st[:, 0], sc[:], AX_X, ALU.max))
                        nc.vector.tensor_tensor(sc[:], sc[:], bc(st[:, 0]), ALU.subtract).then_inc(v_m, 1)
                        dve.wait_ge(a_e, 1)
                        own(nc.vector.tensor_reduce(st[:, 1], ex[:], AX_X, ALU.add))
                        own(nc.vector.reciprocal(st[:, 2], st[:, 1]))
                        nc.vector.tensor_tensor(ex[:], ex[:], bc(st[:, 2]), ALU.mult).then_inc(v_pr, 1)
                        dve.wait_ge(a_t, 1)
                        nc.vector.tensor_tensor(tl[:], ps[:, 1, :].rearrange("p (j k) -> p j k", j=NT), f(th[:]),
                                                ALU.subtract).then_inc(v_t, 1)
                        for j in range(NT):
                            dve.wait_ge(s_y, j + 1)
                            nc.vector.scalar_tensor_tensor(out=x[:, j, :], in0=ps[:, 4 + j, :], scalar=tg[:, 2:3],
                                                           in1=x[:, j, :], op0=ALU.mult, op1=ALU.add)

        def phase_ternary():
            dve_rows, _, _, _, v_xn, _, act_root = layer_norm("q")
            v_own, a_sq, v_q, s_t, a_t, s_y, v_y, a_g, v_ms, a_rr = (
                sem("q_" + n) for n in ("own", "a_sq", "v_q", "s_t", "a_t", "s_y", "v_y", "a_g", "v_ms",
                                         "a_rr"))
            with ExitStack() as ph:
                sq = sb("qsq", [P, NT, D], ctx=ph)
                rn = sb("qrn", [P, NT, D], ctx=ph)
                st = sb("qst", [P, 8, NT], ctx=ph)
                qi = sb("qi", [P, NT, D], BF16, ctx=ph)
                qt = sb("qt", [P, NC, TG], BF16, ctx=ph)
                y = sb("qy", [P, NT, D], ctx=ph)
                with nc.Block() as blk:
                    @blk.scalar
                    def _(act):
                        act_root(act)
                        for j in range(NT):
                            act.wait_ge(v_xn, j + 1)
                            nc.scalar.activation(sq[:, j], xn[:, j], ACT.Square,
                                                 accum_out=st[:, 0, j:j + 1]).then_inc(a_sq, 1)
                        act.wait_ge(v_ms, 1)
                        root(act, st[:, 6], st[:, 1], a_rr, 0)
                        for j in range(NT):
                            act.wait_ge(s_t, j + 1)
                            nc.scalar.copy(qt[:, :, j * P:(j + 1) * P],
                                           ps[:, j, 0:256].bitcast(BF16).rearrange("p (c t) -> p c t", c=NC)).then_inc(a_t, 1)
                        for j in range(NT):
                            act.wait_ge(v_y, j + 1)
                            nc.scalar.activation(sq[:, j], y[:, j], ACT.Gelu).then_inc(a_g, 1)

                    @blk.tensor
                    def _(pe):
                        for j in range(NT):
                            pe.wait_ge(v_q, j + 1)
                            dst = ps[:, j, 0:256].bitcast(BF16)
                            for c in range(NC):
                                last = nc.tensor.transpose(dst[:, c * P:(c + 1) * P], qi[:, j, c * P:(c + 1) * P],
                                                           identb[:])
                            last.then_inc(s_t, 1)
                        for j in range(NT):
                            pe.wait_ge(a_t, j + 1)
                            for c in range(NC):
                                last = nc.tensor.matmul(ps[:, 4 + j, :], qt[:, c, j * P:(j + 1) * P], tern[:, c, :],
                                                        start=(c == 0), stop=(c == NC - 1))
                            last.then_inc(s_y, 1)

                    @blk.vector
                    def _(dve):
                        dve_rows(dve)
                        own = Own(dve, v_own)
                        dve.wait_ge(a_sq, NT)
                        nc.vector.tensor_scalar(st[:, 1], st[:, 0], 1.0 / D, EPS, ALU.mult, ALU.add).then_inc(v_ms, 1)
                        dve.wait_ge(a_rr, 2)
                        newton(own, st[:, 6], st[:, 1], st[:, 7])
                        for j in range(NT):
                            last = nc.vector.tensor_scalar(rn[:, j], xn[:, j], st[:, 6, j:j + 1], None, ALU.mult)
                        own(last)
                        nc.vector.tensor_reduce(st[:, 2], rn[:], AX_X, ALU.max)
                        own(nc.vector.tensor_reduce(st[:, 3], rn[:], AX_X, ALU.min))
                        own(nc.vector.tensor_scalar(st[:, 3], st[:, 3], -1.0, None, ALU.mult))
                        own(nc.vector.tensor_tensor(st[:, 2], st[:, 2], st[:, 3], ALU.max))
                        own(nc.vector.tensor_scalar(st[:, 2], st[:, 2], EPS, None, ALU.max))
                        own(nc.vector.reciprocal(st[:, 4], st[:, 2]))
                        own(nc.vector.tensor_scalar(st[:, 4], st[:, 4], 127.0, None, ALU.mult))
                        own(nc.vector.tensor_scalar(st[:, 5], st[:, 2], wsc[:, 0:1], 1.0 / 127.0, ALU.mult, ALU.mult))
                        for j in range(NT):
                            last = nc.vector.tensor_scalar(rn[:, j], rn[:, j], st[:, 4, j:j + 1], None, ALU.mult)
                        own(last)
                        own(nc.vector.tensor_scalar(rn[:], rn[:], MAGIC, None, ALU.add))
                        own(nc.vector.tensor_scalar(rn[:], rn[:], MAGIC, 127.0, ALU.subtract, ALU.min))
                        for j in range(NT):
                            nc.vector.tensor_scalar(qi[:, j], rn[:, j], -128.0, None, ALU.max).then_inc(v_q, 1)
                        for j in range(NT):
                            dve.wait_ge(s_y, j + 1)
                            nc.vector.scalar_tensor_tensor(out=y[:, j], in0=ps[:, 4 + j, :], scalar=st[:, 5, j:j + 1],
                                                           in1=bf2[:], op0=ALU.mult, op1=ALU.add).then_inc(v_y, 1)
                        for j in range(NT):
                            dve.wait_ge(a_g, j + 1)
                            own(nc.vector.tensor_tensor(y[:, j], xn[:, j], sq[:, j], ALU.add))
                            nc.vector.scalar_tensor_tensor(out=x[:, j, :], in0=y[:, j], scalar=tg[:, 6:7],
                                                           in1=x[:, j, :], op0=ALU.mult, op1=ALU.add)

        def phase_heads(tag, NKV, HP, KEYS, norm, wq, wo, wkv, gate):
            dve_rows, pe_turn, act_high, dve_low, v_xn, v_xl, act_root = layer_norm("h" + tag)
            NS = 2 * HP
            NSTEP = NKV * NS
            NP = NKV * HP
            HB = BG // 2
            SCALE = float(HD) ** -0.5
            names = ("s_q", "a_q", "v_q", "s_k", "a_ksq", "s_kss", "v_kn", "a_k", "v_k", "s_v", "a_v", "v_v", "s_s",
                     "v_s", "v_m", "a_e", "v_p", "s_t", "a_t", "v_t", "s_av", "a_o", "v_o", "s_wo", "a_wq", "p_wq",
                     "a_wo", "p_wo", "a_kv", "p_kv", "l_kv", "v_own", "a_krs", "a_qrs", "p_z", "p_c", "lq0", "lq1", "lo0", "lo1")
            m = {n: sem(f"h{tag}_{n}") for n in names}
            QB, SBK, TBK, AB, OB = 0, 1, 2, 3, 4
            PT = 128 * (HB * KEYS // P)
            with ExitStack() as ph:
                def tb(name, shape, dt=F32):
                    return sb(f"h{tag}_{name}", shape, dt, ctx=ph)
                rq, wqh, wql = tb("rq", [P, 2, NC, 2 * HD]), tb("wqh", [P, 2, NC, 2 * HD], F32R), tb("wql", [P, 2, NC, 2 * HD], F32R)
                ro, woh, wol = tb("ro", [P, 2, 2, D]), tb("woh", [P, 2, 2, D], F32R), tb("wol", [P, 2, 2, D], F32R)
                rk, wkh, wkl = tb("rk", [P, 2, NC, HD]), tb("wkh", [P, 2, NC, HD], F32R), tb("wkl", [P, 2, NC, HD], F32R)
                qh, ql = tb("qh", [P, 2, BG, 2, S], F32R), tb("ql", [P, 2, BG, 2, S], F32R)
                kh, kl = tb("kh", [P, BG, KEYS], F32R), tb("kl", [P, BG, KEYS], F32R)
                vh, vl = tb("vh", [P, BG, HD], F32R), tb("vl", [P, BG, HD], F32R)
                ex, pr = tb("ex", [P, HB, KEYS]), tb("pr", [P, HB, KEYS])
                mx = tb("mx", [P, 6, HB])
                th, tl = tb("th", [P, PT], F32R), tb("tl", [P, PT], F32R)
                oh, ol = tb("oh", [P, 2, HB, S], F32R), tb("ol", [P, 2, HB, S], F32R)
                if norm:
                    sq, ksq, rks, kn, sc = (tb("sq", [P, 2, BG, 2, S]), tb("ksq", [P, TG]), tb("rks", [P, TG]), tb("kn", [P, TG]),
                                            tb("sc", [P, HB, KEYS]))

                    ch, cl = tb("ch", [P, NC, TG], F32R), tb("cl", [P, NC, TG], F32R)

                def ring_of(z, n):
                    return z[:, n // 2, :, n % 2, :]

                def by_batch(bank):
                    return ps[:, bank, :].rearrange("p (b t) -> p b t", t=S)

                def by_head(z):
                    return z[:].rearrange("p h b t -> p b h t")

                def kbank(bank):
                    return ps[:, bank, :].rearrange("p (b k) -> p b k", k=KEYS)

                with nc.Block() as blk:
                    @blk.sync
                    def _(sp):
                        def load_kv(i):
                            wait(sp, m["p_kv"], i)
                            sp.dma_start(rk[:].rearrange("p a c n -> p (a c n)"),
                                         wkv[bass.ds(i, 1)].rearrange("i p n -> (i p) n")).then_inc(m["l_kv"], 16)

                        def load_pair(n, par, w=True):
                            for k, buf, src, ls in (("p_wq", rq, wq, "lq"), ("p_wo", ro, wo, "lo")):
                                if w:
                                    sp.wait_ge(m[k], n - 1)
                                sp.dma_start(buf[:, par].rearrange("p c n -> p (c n)"),
                                             src[bass.ds(n, 1)].rearrange("i p n -> (i p) n")).then_inc(m[f"{ls}{par}"], 16)
                        load_kv(0)
                        load_pair(0, 0, False)
                        load_pair(1, 1, False)
                        load_kv(1)
                        for p in range(2, HP):
                            load_pair(p, p % 2)
                        with sp.Fori(1, NKV - 1) as i:
                            load_kv(i + 1)
                            for p in range(HP):
                                load_pair(i * HP + p, p % 2)
                        for p in range(HP):
                            load_pair((NKV - 1) * HP + p, p % 2)

                    def use(n):
                        return n

                    def split_steps(eng, i, t, last, kv, q, o):
                        if t == 1 and not last:
                            kv(i + 1)
                        if t % 2:
                            mm = (t - 1) // 2
                            if not (last and mm + 2 >= HP):
                                q(i * HP + mm + 2, mm % 2, i * (HP // 2) + (mm + 2) // 2)
                            if not (last and mm + 1 >= HP):
                                o(i * HP + mm + 1, (mm + 1) % 2, i * (HP // 2) + (mm + 1) // 2)

                    def over_groups(eng, body):
                        body(0, True, False)
                        with eng.Fori(1, NKV - 1) as i:
                            body(i, False, False)
                        body(NKV - 1, False, True)

                    @blk.gpsimd
                    def _(pool):
                        if norm:
                            nc.gpsimd.memset(f(vh[:]), 0.0).then_inc(m["p_z"], 1)
                            nc.gpsimd.memset(f(vl[:]), 0.0).then_inc(m["p_z"], 1)
                            for z, src in ((ch, Hh), (cl, Hl)):
                                nc.gpsimd.tensor_copy(z[:].rearrange("p c (b t) -> p (c b) t", t=S),
                                                      f(src[:, :, :, 0, :]).rearrange("p c b t -> p (c b) t")).then_inc(m["p_c"], 1)

                        def kv(i):
                            pool.wait_ge(m["a_kv"], i + 1)
                            nc.gpsimd.tensor_tensor(wkl[:], rk[:], f(wkh[:]), ALU.subtract).then_inc(m["p_kv"], 1)

                        def q(n, par, _):
                            pool.wait_ge(m["a_wq"], n + 1)
                            nc.gpsimd.tensor_tensor(wql[:, par], rq[:, par], f(wqh[:, par]), ALU.subtract).then_inc(m["p_wq"], 1)

                        def o(n, par, _):
                            pool.wait_ge(m["a_wo"], n + 1)
                            nc.gpsimd.tensor_tensor(wol[:, par], ro[:, par], f(woh[:, par]), ALU.subtract).then_inc(m["p_wo"], 1)
                        kv(0)
                        q(0, 0, 0)
                        q(1, 1, 0)
                        o(0, 0, 0)

                        def body(i, first, last):
                            for t in range(NS):
                                split_steps(pool, i, t, last, kv, q, o)
                        over_groups(pool, body)

                    @blk.scalar
                    def _(act):
                        def kv(i):
                            act.wait_ge(m["l_kv"], 16 * (i + 1))
                            wait(act, m["s_v"], i)
                            nc.scalar.copy(wkh[:], rk[:]).then_inc(m["a_kv"], 1)

                        def q(n, par, u):
                            act.wait_ge(m[f"lq{par}"], 16 * (u + 1))
                            wait(act, m["s_q"], 2 * n - 2)
                            nc.scalar.copy(wqh[:, par], rq[:, par]).then_inc(m["a_wq"], 1)

                        def o(n, par, u):
                            act.wait_ge(m[f"lo{par}"], 16 * (u + 1))
                            wait(act, m["s_wo"], 2 * n - 2)
                            nc.scalar.copy(woh[:, par], ro[:, par]).then_inc(m["a_wo"], 1)

                        def keys_high(i):
                            if norm:
                                act.wait_ge(m["v_kn"], i + 1)
                                nc.scalar.copy(kh[:].rearrange("p b k -> p (b k)"), kn[:]).then_inc(m["a_k"], 1)
                            else:
                                act.wait_ge(m["s_k"], i + 1)
                                nc.scalar.copy(kh[:, 0:HB], kbank(QB))
                                nc.scalar.copy(kh[:, HB:BG], kbank(TBK)).then_inc(m["a_k"], 1)

                        def keys_root(i):
                            act.wait_ge(m["s_kss"], i + 1)
                            root(act, rks[:], ps[:, AB, :], m["a_krs"], 2 * i, 1.0 / HD, EPS)

                        def queries_root(n):
                            act.wait_ge(m["s_s"], n + 1)
                            root(act, mx[:, 4], ps[:, SBK, 256:256 + 2 * HB].rearrange("p (b e) -> p b e", e=2)[:, :, 0],
                                 m["a_qrs"], 2 * n, 1.0 / HD, EPS, math.log(SCALE))

                        def keys_square(i):
                            act.wait_ge(m["s_k"], i + 1)
                            nc.scalar.activation(ksq[:], ps[:, TBK, :], ACT.Square).then_inc(m["a_ksq"], 1)

                        def head_high(n, ring):
                            act.wait_ge(m["s_q"], n + 1)
                            if norm:
                                nc.scalar.activation(ring_of(sq, ring), by_batch(QB), ACT.Square)
                            nc.scalar.copy(ring_of(qh, ring), by_batch(QB)).then_inc(m["a_q"], 1)

                        def turned_high(n):
                            act.wait_ge(m["s_t"], n)
                            nc.scalar.copy(th[:], ps[:, TBK, 0:PT]).then_inc(m["a_t"], 1)

                        def out_high(n):
                            act.wait_ge(m["s_av"], n)
                            nc.scalar.copy(by_head(oh), ps[:, AB, :].rearrange("p (b h t) -> p b h t", h=2, t=S)).then_inc(m["a_o"], 1)

                        act_root(act)
                        kv(0)
                        q(0, 0, 0)
                        q(1, 1, 0)
                        o(0, 0, 0)
                        act_high(act)
                        if norm:
                            keys_square(0)
                            keys_root(0)
                        keys_high(0)
                        head_high(0, 0)
                        head_high(1, 1)

                        def body(i, first, last):
                            for t in range(NS):
                                n = i * NS + t
                                if norm:
                                    queries_root(n)
                                act.wait_ge(m["v_m"], n + 1)
                                if not (first and t == 0):
                                    act.wait_ge(m["v_p"], n)
                                if norm:
                                    nc.scalar.activation(ex[:], sc[:], ACT.Exp).then_inc(m["a_e"], 1)
                                else:
                                    for b in range(HB):
                                        ins = nc.scalar.activation(ex[:, b], kbank(SBK)[:, b], ACT.Exp, bias=mx[:, 1, b:b + 1],
                                                                   scale=SCALE, accum_out=mx[:, 2, b:b + 1])
                                    ins.then_inc(m["a_e"], 1)
                                if t == NS - 1 and not last:
                                    if norm:
                                        keys_square(i + 1)
                                    else:
                                        keys_high(i + 1)
                                if not (last and t >= NS - 2):
                                    head_high(n + 2, (t + 2) % 4)
                                if norm and t == NS - 1 and not last:
                                    keys_root(i + 1)
                                if not (first and t == 0):
                                    if norm and t == NS - 1 and not last:
                                        keys_high(i + 1)
                                    turned_high(n)
                                split_steps(act, i, t, last, kv, q, o)
                                if not (first and t == 0):
                                    out_high(n)
                                if t == 0:
                                    act.wait_ge(m["s_v"], i + 1)
                                    if norm:
                                        if first:
                                            act.wait_ge(m["p_z"], 2)
                                        for b in range(2):
                                            r = slice(64 * b, 64 * b + 64)
                                            ins = nc.scalar.copy(vh[r, b::2, :], ps[r, QB, :].rearrange("p (b d) -> p b d", d=HD))
                                    else:
                                        nc.scalar.copy(vh[:, 0:HB].rearrange("p b d -> p (b d)"), ps[:, QB, :])
                                        ins = nc.scalar.copy(vh[:, HB:BG].rearrange("p b d -> p (b d)"), ps[:, TBK, :])
                                    ins.then_inc(m["a_v"], 1)
                        over_groups(act, body)
                        turned_high(NSTEP)
                        out_high(NSTEP)

                    @blk.tensor
                    def _(pe):
                        pe_turn(pe)
                        for j in range(NT):
                            nc.tensor.matmul(ps[:, OB + j, :], zb[:, 0:P], zb[:], start=True, stop=False,
                                             skip_group_check=True)

                        def keys(i):
                            pe.wait_ge(m["p_kv"], i + 1)
                            for half in range(1 if norm else 2):
                                for c in range(NC):
                                    rhs = [(X[:, c, :, 0, :] if norm else
                                            X[:, c, HB * half:HB * half + HB].rearrange("p b s t -> p (b s t)")) for X in (Hh, Hl)]
                                    last = passes(pe, ps[:, TBK if norm or half else QB, :], wkh[:, 0, c], wkl[:, 0, c],
                                                  rhs[0], rhs[1], c == 0, c == NC - 1)
                            last.then_inc(m["s_k"], 1)

                        def keys_sum(i):
                            pe.wait_ge(m["a_ksq"], i + 1)
                            nc.tensor.matmul(ps[:, AB, :], ones[:], ksq[:], start=True, stop=True).then_inc(m["s_kss"], 1)

                        def head(n, hh, ring, par):
                            for c in range(NC):
                                last = passes(pe, ps[:, QB, :], wqh[:, par, c, hh * HD:(hh + 1) * HD],
                                              wql[:, par, c, hh * HD:(hh + 1) * HD], Hh[:, c, :, 1, :], Hl[:, c, :, 1, :],
                                              c == 0, c == NC - 1)
                            last.then_inc(m["s_q"], 1)

                        def scores(t):
                            pair = (t // 2) % 2
                            for b4 in range(HB):
                                b = HB * (t % 2) + b4
                                mine = lambda z: z[:, pair, b].rearrange("p h t -> p (h t)")
                                last = passes(pe, ps[:, SBK, b4 * KEYS:(b4 + 1) * KEYS], mine(qh), mine(ql), kh[:, b], kl[:, b],
                                              True, True)
                                if norm:
                                    last = nc.tensor.matmul(ps[:, SBK, 256 + 2 * b4:258 + 2 * b4], mine(sq), ones[:, 0:2],
                                                            start=True, stop=True)
                            last.then_inc(m["s_s"], 1)

                        def turn():
                            for c in range(PT // P):
                                last = nc.tensor.transpose(ps[:, TBK, c * P:(c + 1) * P],
                                                           pr[:].rearrange("p b k -> p (b k)")[:, c * P:(c + 1) * P], ident[:])
                            last.then_inc(m["s_t"], 1)

                        def values_of(t):
                            for b4 in range(HB):
                                b = HB * (t % 2) + b4
                                c = b4 * KEYS // P
                                last = passes(pe, ps[:, AB, b4 * P:(b4 + 1) * P], vh[:, b], vl[:, b], th[:, c * P:(c + 1) * P],
                                              tl[:, c * P:(c + 1) * P], True, True)
                            last.then_inc(m["s_av"], 1)

                        def output(t, final=False):
                            par = (t // 2) % 2
                            for jj in range(2):
                                for h in range(2):
                                    last = passes(pe, ps[:, OB + 2 * (t % 2) + jj, :], oh[:, h, 2 * jj:2 * jj + 2].rearrange("p b t -> p (b t)"),
                                                  ol[:, h, 2 * jj:2 * jj + 2].rearrange("p b t -> p (b t)"), woh[:, par, h], wol[:, par, h], False,
                                                  final and h == 1, skip_group_check=True)
                            last.then_inc(m["s_wo"], 1)

                        def values():
                            for half in range(1 if norm else 2):
                                for b in range(HB):
                                    for c in range(NC):
                                        lhs = ([z[:, c, b * P:(b + 1) * P] for z in (ch, cl)] if norm else
                                               [z[:, c, HB * half + b].rearrange("p s t -> p (s t)") for z in (Hh, Hl)])
                                        last = passes(pe, ps[:, TBK if half else QB, b * HD:(b + 1) * HD], lhs[0], lhs[1],
                                                      wkh[:, 1, c], wkl[:, 1, c], c == 0, c == NC - 1)
                            last.then_inc(m["s_v"], 1)

                        pe.wait_ge(v_xl, NT)
                        keys(0)
                        if norm:
                            keys_sum(0)
                        pe.wait_ge(m["v_k"], 1)
                        pe.wait_ge(m["p_wq"], 1)
                        head(0, 0, 0, 0)
                        pe.wait_ge(m["v_q"], 1)
                        head(1, 1, 1, 0)

                        def body(i, first, last):
                            for t in range(NS):
                                n = i * NS + t
                                start = first and t == 0
                                if t % 2 == 0:
                                    pe.wait_ge(m["v_q"], n + 2)
                                if t == 0:
                                    pe.wait_ge(m["v_k"], i + 1)
                                if not start:
                                    pe.wait_ge(m["v_s" if norm else "a_e"], n)
                                scores(t)
                                if t == NS - 1 and not last:
                                    pe.wait_ge(m["v_q"], n + 2)
                                    pe.wait_ge(m["v_t"], n - 1)
                                    keys(i + 1)
                                    if not norm:
                                        pe.wait_ge(m["v_k"], i + 2)
                                if t == 1:
                                    pe.wait_ge(m["v_v"], i + 1)
                                if not (last and t >= NS - 2):
                                    pe.wait_ge(m["v_q"], n + 2)
                                    if t % 2 == 0:
                                        pe.wait_ge(m["p_wq"], i * HP + t // 2 + 2)
                                    head(n + 2, t % 2, (t + 2) % 4, ((t + 2) // 2) % 2)
                                if norm and t == NS - 1 and not last:
                                    pe.wait_ge(m["v_o"], n - 1)
                                    keys_sum(i + 1)
                                    pe.wait_ge(m["v_kn"], i + 2)
                                if not start:
                                    pe.wait_ge(m["v_p"], n)
                                    if not (first and t == 1):
                                        pe.wait_ge(m["v_t"], n - 1)
                                    turn()
                                if not (first and t < 2):
                                    pe.wait_ge(m["v_o"], n - 1)
                                    if t % 2 == 0:
                                        pe.wait_ge(m["p_wo"], i * HP + t // 2)
                                    output((t - 2) % NS)
                                if not start:
                                    pe.wait_ge(m["v_t"], n)
                                    values_of((t - 1) % NS)
                                if t == 0:
                                    pe.wait_ge(m["v_q"], n + 3)
                                    if norm and first:
                                        pe.wait_ge(m["p_c"], 2)
                                    values()
                        over_groups(pe, body)
                        pe.wait_ge(m["v_p"], NSTEP)
                        pe.wait_ge(m["v_t"], NSTEP - 1)
                        turn()
                        pe.wait_ge(m["v_o"], NSTEP - 1)
                        pe.wait_ge(m["p_wo"], NP)
                        output(NS - 2, True)
                        pe.wait_ge(m["v_t"], NSTEP)
                        values_of(NS - 1)
                        pe.wait_ge(m["v_o"], NSTEP)
                        output(NS - 1, True)

                    @blk.vector
                    def _(dve):
                        dve_rows(dve)
                        dve_low(dve)

                        def keys_norm(i):
                            dve.wait_ge(m["a_krs"], 2 * i + 2)
                            nc.vector.scalar_tensor_tensor(out=kn[:], in0=ps[:, TBK, :], scalar=qkw[:], in1=rks[:],
                                                           op0=ALU.mult, op1=ALU.mult).then_inc(m["v_kn"], 1)

                        def keys_low(i):
                            dve.wait_ge(m["a_k"], i + 1)
                            if norm:
                                nc.vector.tensor_tensor(kl[:].rearrange("p b k -> p (b k)"), kn[:],
                                                        f(kh[:]).rearrange("p b k -> p (b k)"), ALU.subtract).then_inc(m["v_k"], 1)
                            else:
                                nc.vector.tensor_tensor(kl[:, 0:HB], kbank(QB), f(kh[:, 0:HB]), ALU.subtract)
                                nc.vector.tensor_tensor(kl[:, HB:BG], kbank(TBK), f(kh[:, HB:BG]), ALU.subtract).then_inc(m["v_k"], 1)

                        def head_low(n, ring):
                            dve.wait_ge(m["a_q"], n + 1)
                            nc.vector.tensor_tensor(ring_of(ql, ring), by_batch(QB), f(ring_of(qh, ring)), ALU.subtract).then_inc(m["v_q"], 1)

                        def turned_low(n):
                            dve.wait_ge(m["a_t"], n)
                            nc.vector.tensor_tensor(tl[:], ps[:, TBK, 0:PT], f(th[:]), ALU.subtract).then_inc(m["v_t"], 1)

                        def out_low(n):
                            dve.wait_ge(m["a_o"], n)
                            nc.vector.tensor_tensor(by_head(ol), ps[:, AB, :].rearrange("p (b h t) -> p b h t", h=2, t=S),
                                                    f(by_head(oh)), ALU.subtract).then_inc(m["v_o"], 1)

                        bc = lambda y: y.unsqueeze(2).broadcast_to((P, HB, KEYS))

                        def largest(n, own):
                            dve.wait_ge(m["s_s"], n + 1)
                            if norm:
                                dve.wait_ge(m["a_qrs"], 2 * n + 2)
                                nc.vector.tensor_tensor(sc[:], kbank(SBK)[:, 0:HB], bc(mx[:, 4]), ALU.mult).then_inc(m["v_s"], 1)
                                dve.wait_ge(m["v_s"], n + 1)
                                own(nc.vector.tensor_tensor(sc[:], sc[:], mask3[:].unsqueeze(1).broadcast_to((P, HB, KEYS)), ALU.add))
                                own(nc.vector.tensor_reduce(mx[:, 0], sc[:], AX_X, ALU.max))
                                nc.vector.tensor_tensor(sc[:], sc[:], bc(mx[:, 0]), ALU.subtract).then_inc(m["v_m"], 1)
                            else:
                                own(nc.vector.tensor_reduce(mx[:, 0], kbank(SBK), AX_X, ALU.max))
                                nc.vector.tensor_scalar(mx[:, 1], mx[:, 0], -SCALE, None, ALU.mult).then_inc(m["v_m"], 1)

                        def shares(n, own, start):
                            dve.wait_ge(m["a_e"], n + 1)
                            if norm:
                                own(nc.vector.tensor_reduce(mx[:, 2], ex[:], AX_X, ALU.add))
                            own(nc.vector.reciprocal(mx[:, 5], mx[:, 2]))
                            if not start:
                                dve.wait_ge(m["s_t"], n)
                            nc.vector.tensor_tensor(pr[:], ex[:], bc(mx[:, 5]), ALU.mult).then_inc(m["v_p"], 1)

                        if norm:
                            keys_norm(0)
                        keys_low(0)
                        head_low(0, 0)
                        head_low(1, 1)
                        per_step = 4 if norm else 2

                        def body(i, first, last):
                            own = Own(dve, m["v_own"], per_step * NS * i)
                            for t in range(NS):
                                n = i * NS + t
                                start = first and t == 0
                                largest(n, own)
                                if t == NS - 1 and not last and not norm:
                                    keys_low(i + 1)
                                if not (last and t >= NS - 2):
                                    head_low(n + 2, (t + 2) % 4)
                                if t == NS - 1 and not last and norm:
                                    keys_norm(i + 1)
                                    keys_low(i + 1)
                                if not start:
                                    turned_low(n)
                                shares(n, own, start)
                                if not start:
                                    out_low(n)
                                if t == 0:
                                    dve.wait_ge(m["a_v"], i + 1)
                                    if norm:
                                        for b in range(2):
                                            r = slice(64 * b, 64 * b + 64)
                                            ins = nc.vector.tensor_tensor(vl[r, b::2, :], ps[r, QB, :].rearrange("p (b d) -> p b d", d=HD),
                                                                          f(vh[r, b::2, :]), ALU.subtract)
                                    else:
                                        nc.vector.tensor_tensor(vl[:, 0:HB].rearrange("p b d -> p (b d)"), ps[:, QB, :],
                                                                f(vh[:, 0:HB]).rearrange("p b d -> p (b d)"), ALU.subtract)
                                        ins = nc.vector.tensor_tensor(vl[:, HB:BG].rearrange("p b d -> p (b d)"), ps[:, TBK, :],
                                                                      f(vh[:, HB:BG]).rearrange("p b d -> p (b d)"), ALU.subtract)
                                    ins.then_inc(m["v_v"], 1)
                            assert own.n == per_step * NS, own.n
                        over_groups(dve, body)
                        turned_low(NSTEP)
                        out_low(NSTEP)
                        dve.wait_ge(m["s_wo"], NSTEP)
                        for j in range(NT):
                            nc.vector.scalar_tensor_tensor(out=x[:, j, :], in0=ps[:, OB + j, :], scalar=tg[:, gate:gate + 1],
                                                           in1=x[:, j, :], op0=ALU.mult, op1=ALU.add)

        end_phase()
        with nc.Fori(0, groups) as g:
            for n, phase in enumerate((
                    lambda: phase_load(g),
                    phase_local,
                    lambda: phase_mixture("0", "top2", D, E8, a["L0_wcat"], a["L0_B"], bbase["0"]),
                    lambda: phase_heads("1", 4, 4, 2 * S, False, a["L1_Wq"], a["L1_Wo"], a["L1_Wkv"], 1),
                    lambda: phase_mixture("1", "threshold", D, E8 + 2, a["L1_wcat"], a["L1_B"], bbase["1"]),
                    phase_text,
                    phase_ternary,
                    lambda: phase_heads("3", 8, 2, S, True, a["L3_Wq"], a["L3_Wo"], a["L3_Wkv"], 3),
                    lambda: phase_mixture("3", "softmax", 0, E8, a["L3_wcat"], a["L3_B"], None))):
                if n <= stages:
                    phase()
                    end_phase()
            l_out = sem("l_out")
            with nc.Block() as blk:
                @blk.sync
                def _(sp):
                    sp.dma_start(out[bass.ds(g, 1)].rearrange("a p t d -> (a p) t d"), x[:]).then_inc(l_out, 16)
                    sp.wait_ge(l_out, 16)
            end_phase()


def constants():
    r = np.arange(P)
    head, query = r // TB, r % TB
    key = np.arange(KW)
    gap = key[None, :] - query[:, None]
    v = np.zeros((8, 4, KW), np.float32)
    for q in range(8):
        for t in range(4):
            pos = (4 * q + t) * TB - WIN // 2 + key
            v[q, t] = (pos >= 0) & (pos < D)
    return {
        "c_ident": np.eye(P, dtype=np.float32),
        "c_hmask": ((r[:, None] % S) // HD0 == np.arange(HEADS0)[None, :]).astype(np.float32),
        "c_band": np.where((gap >= 0) & (gap < WIN), 0.0, -1e30).astype(np.float32),
        "c_omask": (np.arange(S)[None, :] // HD0 == head[:, None]).astype(np.float32),
        "c_osel": (query[:, None] == np.arange(TB)[None, :]).astype(np.float32),
        "c_bmask": np.where(r[:, None] // S == r[None, :] // S, 0.0, -1e30).astype(np.float32),
        "c_vrow": v.reshape(1, 8 * P),
    }


def layouts(i):
    def rows(z):
        return z.reshape(G, NT, P, D).transpose(0, 2, 1, 3)

    def chunks(z):
        return z.reshape(NC, P, -1).transpose(1, 0, 2)

    def pairs_in(z):
        return z.reshape(NC, P, -1, 2 * HD).transpose(2, 1, 0, 3).reshape(-1, P, NC * 2 * HD)

    def pairs_out(z):
        return z.reshape(-1, 2, HD, D).transpose(0, 2, 1, 3).reshape(-1, P, 2 * D)

    def keys_values(k, v):
        both = np.stack([k, v]).reshape(2, NC, P, -1, HD)
        return both.transpose(3, 2, 0, 1, 4).reshape(-1, P, 2 * NC * HD)

    def second(z):
        return z.transpose(0, 2, 1).reshape(E8 * R16, D)

    def first(*parts):
        return chunks(np.concatenate([p.reshape(-1, D).T for p in parts], axis=1))

    d = {
        "x": rows(i["x"]), "ctx": rows(i["ctx_4096"]),
        "ctxT": i["ctx_4096"].reshape(G, TG, NC, P).transpose(0, 3, 2, 1),
        "mask": i["mask_1x1xSxS2_ff0"].reshape(S, S),
        "g_xattn": i["g_xattn"], "g_ffn": i["g_ffn"],
        "L0_wcat": first(i["L0_ffn_W_base"], i["L0_ffn_A"], i["L0_ffn_W_router"]),
        "L0_B": second(i["L0_ffn_B"]),
        "L1_Wq": pairs_in(i["L1_xattn_Wq"]), "L1_Wo": pairs_out(i["L1_xattn_Wo"]),
        "L1_Wkv": keys_values(i["L1_xattn_Wk"], i["L1_xattn_Wv"]),
        "L1_wcat": first(i["L1_ffn_W_base"], i["L1_ffn_A"], i["L1_ffn_W_gate"], i["L1_ffn_W_thr"], i["L1_ffn_W_thr"]),
        "L1_B": second(i["L1_ffn_B"]),
        "L2_WqT": chunks(i["L2_xattn_Wq"].T), "L2_WkT": chunks(i["L2_xattn_Wk"].T),
        "L2_bq": i["L2_xattn_bq"].reshape(NC, P).T, "L2_bk": i["L2_xattn_bk"].reshape(NC, P).T,
        "L2_ffn_WT": chunks(i["L2_ffn_W"].T),
        "L3_Wq": pairs_in(i["L3_xattn_Wq"].T), "L3_Wo": pairs_out(i["L3_xattn_Wo"].T),
        "L3_Wkv": keys_values(i["L3_xattn_Wk"].T, i["L3_xattn_Wv"].T),
        "L3_wcat": first(i["L3_ffn_A"], i["L3_ffn_Wr"]),
        "L3_B": second(i["L3_ffn_B"]),
    }
    for n in ("q", "k", "v", "o"):
        d[f"L0_W{n}T"] = i[f"L0_xattn_W{n}"].T
    for n in ("L0_xattn_bq", "L0_xattn_bk", "L0_xattn_bv", "L0_xattn_bo", "L0_ffn_b_base", "L1_ffn_b_base",
              "L1_ffn_b_thr", "L3_ffn_br", "L2_ffn_b", "L3_xattn_q_norm_w", "L3_xattn_k_norm_w"):
        d[n] = i[n]
    d.update(constants())
    return {n: np.ascontiguousarray(z) for n, z in d.items()}


def kernel(**inputs):
    import concourse.bacc as bacc
    from concourse.bass_utils import run_bass_kernel_spmd

    nc = bacc.Bacc("TRN2", target_bir_lowering=False, num_devices=1)
    arrays, aps = {}, {}
    for name, z in layouts({n: np.asarray(v) for n, v in inputs.items()}).items():
        arrays[f"in_{name}"] = z
        aps[name] = nc.dram_tensor(f"in_{name}", z.shape, mybir.dt.from_np(z.dtype), kind="ExternalInput").ap()
    out = nc.dram_tensor("out_rows", (G, P, NT, D), F32, kind="ExternalOutput").ap()
    build(nc, aps, out)
    r = run_bass_kernel_spmd(nc, [arrays], core_ids=[0])
    return r.results[0]["out_rows"].transpose(0, 2, 1, 3).reshape(B, S, D)
```

```python
import math
from contextlib import ExitStack

import numpy as np

import concourse.bass as bass
from concourse import mybir

F32 = mybir.dt.float32
F32R = mybir.dt.float32r
BF16 = mybir.dt.bfloat16
ALU = mybir.AluOpType
ACT = mybir.ActivationFunctionType
AX_X = mybir.AxisListType.X

P = 128
B, S, D = 32, 64, 512
BG = 8
G = B // BG
TG = BG * S
NT = TG // P
NC = D // P
EPS = 1e-5
BIG = 3.0e38
LN_EXP = "natural_log_exp_and_others"
MAGIC = 12582912.0
LORA_SCALE = 2.0
E8, R16 = 8, 16
HEADS0, HD0, WIN = 8, 8, 16
TB = 16
KW = 2 * TB
PADT = WIN // 2 + D + WIN // 2
HD = 128


def wait(eng, sem, value):
    if type(value) is int and value <= 0:
        return
    eng.wait_ge(sem, value)


class Own:

    def __init__(self, eng, sem, base=0):
        self.eng, self.sem, self.base, self.n = eng, sem, base, 0

    def __call__(self, ins):
        self.n += 1
        ins.then_inc(self.sem, 1)
        self.eng.wait_ge(self.sem, self.base + self.n)


def build(nc, a, out, groups=G):
    with ExitStack() as top:
        def sb(name, shape, dt=F32, ctx=top):
            return ctx.enter_context(nc.sbuf_tensor(name, shape, dt))

        live = []

        def sem(name):
            if not live:
                live.append(ExitStack())
            s = live[0].enter_context(nc.semaphore(name))
            live.append(s)
            return s

        def end_phase():
            nums = sorted(s.num for s in live[1:])
            runs = []
            for n in nums:
                if runs and runs[-1][1] == n:
                    runs[-1][1] = n + 1
                else:
                    runs.append([n, n + 1])
            with nc.Block() as blk:
                @blk.gpsimd
                def _(pool):
                    for first, stop in runs:
                        nc.gpsimd.sem_clear(range(first, stop))
            live[0].close()
            live.clear()

        ps = top.enter_context(nc.psum_tensor("ps", [P, 8, 512], F32))
        x = sb("x", [P, NT, D])
        xn = sb("xn", [P, NT, D])
        cnat = sb("cnat", [P, NT, D])
        Hh = sb("Hh", [P, NC, BG, 2, S], F32R)
        Hl = sb("Hl", [P, NC, BG, 2, S], F32R)
        bst = sb("bst", [P, NT, 6])
        mv = sb("mv", [P, NT, 2])
        rstd = sb("rstd", [P, NT])
        nt = sb("nt", [P, 2, NT])
        ident = sb("ident", [P, P])
        ones = sb("ones", [P, P])
        zb = sb("zb", [P, 512], BF16)
        identb = sb("identb", [P, P], BF16)
        hmask = sb("hmask", [P, HEADS0])
        band = sb("band", [P, KW])
        omask = sb("omask", [P, S])
        osel = sb("osel", [P, TB])
        bmask = sb("bmask", [P, P])
        vrow = sb("vrow", [1, 8, P])
        gates = sb("gates", [P, 8])
        tg = sb("tg", [P, 8])
        wbd = {n: sb("bd_" + n, [P, P]) for n in ("q", "k", "v", "o")}
        b0 = {n: sb("b0_" + n, [P, 1]) for n in ("q", "k", "o")}
        bvrow = sb("bvrow", [1, P])
        bbase = {n: sb("bbase_" + n, [1, D]) for n in ("0", "1")}
        bthr = sb("bthr", [P, 1])
        nbthr = sb("nbthr", [P, 1])
        br3 = sb("br3", [P, E8])
        bq2 = sb("bq2", [P, NC])
        bk2 = sb("bk2", [P, NC])
        bf2 = sb("bf2", [P, D])
        tern = sb("tern", [P, NC, D], BF16)
        wmean = sb("wmean", [P, 1])
        wsc = sb("wsc", [P, 4])
        mask3 = sb("mask3", [P, S])
        nw3 = sb("nw3", [P, 2])
        qkw = sb("qkw", [P, 1])

        def f(ap):
            return ap.bitcast(F32)

        l_c = sem("l_c")
        c_v = sem("c_v")
        c_a = sem("c_a")
        c_p = sem("c_p")
        c_z = sem("c_z")
        with ExitStack() as ph:
            wt = sb("wt", [P, NC, D], ctx=ph)
            wab = sb("wab", [P, NC, D], ctx=ph)
            loads = []
            for t, n in ((ident, "c_ident"), (hmask, "c_hmask"), (band, "c_band"), (omask, "c_omask"),
                         (osel, "c_osel"), (bmask, "c_bmask")):
                loads.append((t[:], a[n]))
            loads.append((vrow[:].rearrange("a q p -> a (q p)"), a["c_vrow"]))
            loads.append((gates[:, 0:4], a["g_xattn"].unsqueeze(0).broadcast_to((P, 4))))
            loads.append((gates[:, 4:8], a["g_ffn"].unsqueeze(0).broadcast_to((P, 4))))
            for n in ("q", "k", "v", "o"):
                for b in range(2):
                    loads.append((("bd", n, b), a[f"L0_W{n}T"]))
            for b in range(2):
                for n in ("q", "k", "o"):
                    loads.append((b0[n][64 * b:64 * b + 64, :], a[f"L0_xattn_b{n}"].unsqueeze(1)))
                loads.append((bvrow[:, 64 * b:64 * b + 64], a["L0_xattn_bv"].unsqueeze(0)))
                loads.append((mask3[64 * b:64 * b + 64, :], a["mask"]))
            loads.append((bbase["0"][:], a["L0_ffn_b_base"].unsqueeze(0)))
            loads.append((bbase["1"][:], a["L1_ffn_b_base"].unsqueeze(0)))
            loads.append((bthr[:], a["L1_ffn_b_thr"].unsqueeze(0).broadcast_to((P, 1))))
            loads.append((br3[:], a["L3_ffn_br"].unsqueeze(0).broadcast_to((P, E8))))
            loads.append((bq2[:], a["L2_bq"]))
            loads.append((bk2[:], a["L2_bk"]))
            loads.append((bf2[:], a["L2_ffn_b"].unsqueeze(0).broadcast_to((P, D))))
            loads.append((nw3[:, 0:1], a["L3_xattn_q_norm_w"].unsqueeze(1)))
            loads.append((nw3[:, 1:2], a["L3_xattn_k_norm_w"].unsqueeze(1)))
            loads.append((wt[:], a["L2_ffn_WT"]))
            with nc.Block() as blk:
                @blk.sync
                def _(sp):
                    sp.wait_ge(c_z, 4)
                    for dst, src in loads:
                        if type(dst) is tuple:
                            _, n, b = dst
                            dst = wbd[n][64 * b:64 * b + 64, 64 * b:64 * b + 64]
                        sp.dma_start(dst, src).then_inc(l_c, 16)

                @blk.gpsimd
                def _(pool):
                    for n in ("q", "k", "v", "o"):
                        nc.gpsimd.memset(wbd[n][:], 0.0).then_inc(c_z, 1)
                    nc.gpsimd.memset(ones[:], 1.0).then_inc(c_p, 1)
                    nc.gpsimd.memset(zb[:], 0.0).then_inc(c_p, 1)

                @blk.scalar
                def _(act):
                    act.wait_ge(l_c, 16 * len(loads))
                    nc.scalar.activation(tg[:], gates[:], ACT.Tanh).then_inc(c_a, 1)
                    nc.scalar.activation(wab[:], wt[:], ACT.Abs, accum_out=wmean[:]).then_inc(c_a, 1)
                    nc.scalar.preload_act_table_set(LN_EXP)

                @blk.tensor
                def _(pe):
                    pe.wait_ge(c_p, 2)
                    pe.wait_ge(c_a, 2)
                    nc.tensor.matmul(ps[:, 0, 0:1], ones[:], wmean[:], start=True, stop=True).then_inc(c_p, 1)

                @blk.vector
                def _(dve):
                    own = Own(dve, c_v)
                    dve.wait_ge(l_c, 16 * len(loads))
                    own(nc.vector.tensor_copy(identb[:], ident[:]))
                    own(nc.vector.tensor_scalar(nbthr[:], bthr[:], -1.0, None, ALU.mult))
                    own(nc.vector.tensor_tensor(qkw[:], nw3[:, 0:1], nw3[:, 1:2], ALU.mult))
                    dve.wait_ge(c_p, 3)
                    own(nc.vector.tensor_scalar(wsc[:, 0:1], ps[:, 0, 0:1], 1.0 / (D * D), EPS, ALU.mult, ALU.max))
                    own(nc.vector.reciprocal(wsc[:, 1:2], wsc[:, 0:1]))
                    own(nc.vector.tensor_scalar(wab[:], wt[:], wsc[:, 1:2], None, ALU.mult))
                    own(nc.vector.tensor_scalar(wab[:], wab[:], MAGIC, None, ALU.add))
                    own(nc.vector.tensor_scalar(wab[:], wab[:], MAGIC, -1.0, ALU.subtract, ALU.max))
                    own(nc.vector.tensor_scalar(tern[:], wab[:], 1.0, None, ALU.min))

        def root(act, dst, src, own, done, scale=1.0, bias=0.0, factor=0.0):
            nc.scalar.activation(dst, src, ACT.Ln, scale=scale, bias=bias).then_inc(own, 1)
            act.wait_ge(own, done + 1)
            nc.scalar.activation(dst, dst, ACT.Exp, scale=-0.5, bias=factor).then_inc(own, 1)

        def newton(own, y, v, t):
            own(nc.vector.tensor_tensor(t, y, y, ALU.mult))
            own(nc.vector.tensor_tensor(t, t, v, ALU.mult))
            own(nc.vector.tensor_scalar(t, t, -0.5, 1.5, ALU.mult, ALU.add))
            own(nc.vector.tensor_tensor(y, y, t, ALU.mult))

        def layer_norm(tag, flat=None):
            v_own, v_xn, s_xt, a_xh, v_xl, a_rs = (
                sem(f"{n}_{tag}") for n in ("v_lnown", "v_xn", "s_xt", "a_xh", "v_xl", "a_rs"))

            def dve_rows(dve, loads=None):
                own = Own(dve, v_own)
                for j in range(NT):
                    if loads:
                        dve.wait_ge(loads[j], 16)
                    last = nc.vector.bn_stats(bst[:, j, :], x[:, j, :])
                own(last)
                for j in range(NT):
                    last = nc.vector.bn_aggr(mv[:, j, :], bst[:, j, :])
                own(last)
                own(nc.vector.tensor_scalar(nt[:, 0], mv[:, :, 1], EPS, None, ALU.add))
                dve.wait_ge(a_rs, 2)
                newton(own, rstd[:], nt[:, 0], nt[:, 1])
                for j in range(NT):
                    nc.vector.tensor_scalar(xn[:, j, :], x[:, j, :], mv[:, j, 0:1], rstd[:, j:j + 1],
                                            ALU.subtract, ALU.mult).then_inc(v_xn, 1)

            def act_root(act):
                act.wait_ge(v_own, 3)
                root(act, rstd[:], nt[:, 0], a_rs, 0)

            def pe_turn(pe):
                for j in range(NT):
                    pe.wait_ge(v_xn, j + 1)
                    for c in range(NC):
                        last = nc.tensor.transpose(ps[:, j, c * P:(c + 1) * P], xn[:, j, c * P:(c + 1) * P], ident[:])
                    last.then_inc(s_xt, 1)

            def place(part, j):
                if flat:
                    return flat[part][:, :, j * P:(j + 1) * P]
                return (Hh, Hl)[part][:, :, 2 * j:2 * j + 2, 1, :]

            def cols(j):
                if flat:
                    return ps[:, j, :].rearrange("p (c t) -> p c t", c=NC)
                return ps[:, j, :].rearrange("p (c b t) -> p c b t", c=NC, b=2)

            def act_high(act, tiles=range(NT)):
                for j in tiles:
                    act.wait_ge(s_xt, j + 1)
                    nc.scalar.copy(place(0, j), cols(j)).then_inc(a_xh, 1)

            def dve_low(dve, tiles=range(NT)):
                for j in tiles:
                    dve.wait_ge(a_xh, j + 1)
                    nc.vector.tensor_tensor(place(1, j), cols(j), f(place(0, j)), ALU.subtract).then_inc(v_xl, 1)

            return dve_rows, pe_turn, act_high, dve_low, v_xn, v_xl, act_root

        def passes(pe, dst, lh, ll, rh, rl, start, stop, **kw):
            nc.tensor.matmul(dst, lh, rh, start=start, stop=False, **kw)
            nc.tensor.matmul(dst, lh, rl, start=False, stop=False, **kw)
            return nc.tensor.matmul(dst, ll, rh, start=False, stop=stop, **kw)

        def phase_local(g):
            dve_rows, _, _, _, v_xn, _, act_root = layer_norm("l0")
            p_z, a_cp, s_p, a_q, a_k, p_qx, v_qx, a_vx = (
                sem(n) for n in ("p_z", "a_cp", "s_p", "a_q", "a_k", "p_qx", "v_qx", "a_vx"))
            s_s, v_s, v_sub, a_e, v_pr, s_t, a_t, s_av, v_om, s_sel, a_o, s_wo, v_x = (
                sem("o_" + n) for n in ("s_s", "v_s", "v_sub", "a_e", "v_pr", "s_t", "a_t", "s_av", "v_om", "s_sel",
                                        "a_o", "s_wo", "v_x"))
            v_own = sem("o_own")
            l_x = [sem(f"l_x{j}") for j in range(NT)]
            l_c, l_ct, a_ct = sem("l_c"), sem("l_ct"), sem("a_ct")
            NQ = 4
            NB = D // TB // NQ
            SC = float(HD0) ** -0.5
            with ExitStack() as ph:
                craw = sb("craw", [P, NC, BG, S], ctx=ph)
                qx = sb("qx", [P, D // TB, HEADS0, TB], ctx=ph)
                qs = sb("qs", [P, D], ctx=ph)
                kp = sb("kp", [P, 2, PADT], ctx=ph)
                cp = sb("cp", [P, PADT], ctx=ph)
                cw = sb("cw", [P, D // TB, KW], ctx=ph)
                vx = sb("vx", [P, 8, 2, 4, S], ctx=ph)
                sc = sb("sc", [P, 2, NB, KW], ctx=ph)
                ex = sb("ex", [P, 2, NB, KW], ctx=ph)
                pr = sb("pr", [P, 2, NB, KW], ctx=ph)
                st = sb("st", [P, 3, 2, NB], ctx=ph)
                at = sb("at", [P, 4, P], ctx=ph)
                om = sb("om", [P, NB, 2, S], ctx=ph)
                oc = sb("oc", [P, D], ctx=ph)
                tmp = sb("tmp", [P, D], ctx=ph)
                SB_, TBK, AB, CB, PB = 0, 2, 3, 5, 6
                sv = ps[:, SB_, :].rearrange("p (n b k) -> p b n k", n=NB, b=2)
                with nc.Block() as blk:
                    def over_tiles(eng, body):
                        body(0, True, False)
                        with eng.Fori(1, NT - 1) as j:
                            body(j, False, False)
                        body(NT - 1, False, True)

                    def tile_of(z, j):
                        return z[:, bass.ds(j, 1), :].rearrange("p a d -> p (a d)")

                    @blk.sync
                    def _(sp):
                        one = lambda n: a[n][bass.ds(g, 1)].rearrange("a p t d -> (a p) t d")
                        for j in range(NT):
                            sp.dma_start(x[:, j], one("x")[:, j]).then_inc(l_x[j], 16)
                        sp.dma_start(cnat[:], one("ctx")).then_inc(l_c, 16)
                        sp.dma_start(craw[:].rearrange("p c b t -> p c (b t)"), one("ctxT")).then_inc(l_ct, 16)

                    @blk.gpsimd
                    def _(pool):
                        nc.gpsimd.memset(kp[:], 0.0).then_inc(p_z, 1)
                        nc.gpsimd.memset(cp[:], 0.0).then_inc(p_z, 1)
                        nc.gpsimd.memset(vx[:], 0.0).then_inc(p_z, 1)

                        def queries(j, first=False):
                            pool.wait_ge(a_q, j + 1)
                            if not first:
                                pool.wait_ge(s_s, NQ * j)
                            for h in range(HEADS0 // 2):
                                last = nc.gpsimd.tensor_tensor(
                                    qx[:, :, h, :], qs[:].rearrange("p (n t) -> p n t", t=TB),
                                    hmask[:, h:h + 1].unsqueeze(2).broadcast_to((P, D // TB, TB)), ALU.mult)
                            last.then_inc(p_qx, 1)

                        queries(0, True)
                        for c in range(NC):
                            pool.wait_ge(a_ct, c + 1)
                            nc.gpsimd.tensor_tensor(Hl[:, c, :, 0, :], craw[:, c], f(Hh[:, c, :, 0, :]), ALU.subtract)
                        with pool.Fori(1, NT) as j:
                            queries(j)

                    @blk.tensor
                    def _(pe):
                        def queries(j, start=False):
                            pe.wait_ge(v_xn, j + 1)
                            if not start:
                                pe.wait_ge(v_x, j - 1)
                            nc.tensor.matmul(ps[:, PB, :], wbd["q"][:], tile_of(xn, j), start=True, stop=True).then_inc(s_p, 1)

                        def keys(j):
                            pe.wait_ge(a_cp, 2 * j + 2)
                            nc.tensor.matmul(ps[:, PB + 1, :], wbd["k"][:], cp[:, WIN // 2:WIN // 2 + D],
                                             start=True, stop=True).then_inc(s_p, 1)

                        def value_rows(j):
                            pe.wait_ge(a_q, j + 1)
                            pe.wait_ge(a_k, j + 1)
                            for q in range(8):
                                window = cw[:, 4 * q:4 * q + 4, :].rearrange("p n k -> p (n k)")
                                dst = ps[:, PB + q // 4, (q % 4) * P:(q % 4 + 1) * P]
                                nc.tensor.matmul(dst, window, wbd["v"][:], start=True, stop=False)
                                last = nc.tensor.matmul(dst, vrow[:, q, :], bvrow[:], start=False, stop=True)
                            last.then_inc(s_p, 1)

                        def scores(j, n, start):
                            if n == 0:
                                pe.wait_ge(p_qx, j + 1)
                                pe.wait_ge(v_qx, j + 1)
                                pe.wait_ge(a_k, j + 1)
                            if not start:
                                pe.wait_ge(v_s, NQ * j + n)
                            for t in range(NB):
                                t0 = (n * NB + t) * TB
                                last = nc.tensor.matmul(
                                    ps[:, SB_, 2 * t * KW:2 * (t + 1) * KW],
                                    qx[:, n * NB + t].rearrange("p h t -> p (h t)"), kp[:, :, t0:t0 + KW], start=True, stop=True)
                            last.then_inc(s_s, 1)

                        def turn(g, start):
                            pe.wait_ge(v_pr, g + 1)
                            if not start:
                                pe.wait_ge(a_t, g)
                            for b in range(2):
                                for q in range(2):
                                    last = nc.tensor.transpose(
                                        ps[:, TBK, (2 * b + q) * P:(2 * b + q + 1) * P],
                                        pr[:, b, 4 * q:4 * q + 4, :].rearrange("p n k -> p (n k)"), ident[:])
                            last.then_inc(s_t, 1)

                        def values(g, n, start):
                            pe.wait_ge(a_t, g + 1)
                            if not start:
                                pe.wait_ge(v_om, g)
                            for b in range(2):
                                for q in range(2):
                                    last = nc.tensor.matmul(
                                        ps[:, AB + b, q * 256:(q + 1) * 256], at[:, 2 * b + q, :],
                                        vx[:, 2 * n + q, b].rearrange("p n o -> p (n o)"), start=True, stop=True)
                            last.then_inc(s_av, 1)

                        def pick(g, n):
                            pe.wait_ge(v_om, g + 1)
                            for t in range(NB):
                                col = (n * NB + t) * TB
                                last = nc.tensor.matmul(ps[:, CB, col:col + TB],
                                                        om[:, t].rearrange("p b o -> p (b o)"), osel[:],
                                                        start=True, stop=True)
                            last.then_inc(s_sel, 1)

                        def output(j):
                            pe.wait_ge(a_o, j + 1)
                            nc.tensor.matmul(ps[:, PB, :], wbd["o"][:], oc[:], start=True, stop=True).then_inc(s_wo, 1)

                        queries(0, True)
                        keys(0)
                        value_rows(0)

                        def body(j, first, last):
                            for n in range(NQ):
                                g = NQ * j + n
                                scores(j, n, first and n == 0)
                                if not (first and n == 0):
                                    turn(g - 1, first and n == 1)
                                if not (first and n < 2):
                                    pick(g - 2, (n - 2) % NQ)
                                if n == 1:
                                    pe.wait_ge(a_vx, j + 1)
                                if not (first and n == 0):
                                    values(g - 1, (n - 1) % NQ, first and n == 1)
                                if n == 1 and not first:
                                    output(j - 1)
                                if n == 2 and not last:
                                    queries(j + 1, first)
                                    keys(j + 1)
                                if n == 3 and not last:
                                    value_rows(j + 1)

                        over_tiles(pe, body)
                        turn(NQ * NT - 1, False)
                        pick(NQ * NT - 2, NQ - 2)
                        values(NQ * NT - 1, NQ - 1, False)
                        pick(NQ * NT - 1, NQ - 1)
                        output(NT - 1)

                    @blk.scalar
                    def _(act):
                        def context(j, start=False):
                            if not start:
                                act.wait_ge(s_p, 3 * j)
                            nc.scalar.copy(cp[:, WIN // 2:WIN // 2 + D], tile_of(cnat, j)).then_inc(a_cp, 1)
                            act.wait_ge(a_cp, 2 * j + 1)
                            nc.scalar.copy(cw[:], bass.AP(cp[:].tensor, 0, [[PADT, P], [TB, D // TB], [1, KW]])).then_inc(a_cp, 1)

                        def queries_out(j, start=False):
                            act.wait_ge(s_p, 3 * j + 1)
                            if not start:
                                act.wait_ge(p_qx, j)
                                act.wait_ge(v_qx, j)
                            nc.scalar.activation(qs[:], ps[:, PB, :], ACT.Identity, bias=b0["q"][:]).then_inc(a_q, 1)

                        def keys_out(j, start=False):
                            act.wait_ge(s_p, 3 * j + 2)
                            if not start:
                                act.wait_ge(s_s, NQ * j)
                            for b in range(2):
                                r = slice(64 * b, 64 * b + 64)
                                last = nc.scalar.activation(kp[r, b, WIN // 2:WIN // 2 + D], ps[r, PB + 1, :], ACT.Identity,
                                                            bias=b0["k"][r])
                            last.then_inc(a_k, 1)

                        def values_out(j, start):
                            act.wait_ge(s_p, 3 * j + 3)
                            if not start:
                                act.wait_ge(s_av, NQ * j)
                            for t in range(4):
                                r = slice(32 * t, 32 * t + 32)
                                last = nc.scalar.copy(
                                    vx[r, :, :, t, :],
                                    ps[r, PB:PB + 2, :].rearrange("p a (q b o) -> p (a q) b o", q=4, b=2))
                            last.then_inc(a_vx, 1)

                        def powers(g):
                            act.wait_ge(v_sub, g + 1)
                            nc.scalar.activation(ex[:], sc[:], ACT.Exp, scale=SC).then_inc(a_e, 1)

                        def turned(g):
                            act.wait_ge(s_t, g + 1)
                            nc.scalar.copy(at[:], ps[:, TBK, :].rearrange("p (n k) -> p n k", n=4)).then_inc(a_t, 1)

                        def picked(j):
                            act.wait_ge(s_sel, NQ * (j + 1))
                            nc.scalar.copy(oc[:], ps[:, CB, :]).then_inc(a_o, 1)

                        act_root(act)
                        act.wait_ge(p_z, 2)
                        act.wait_ge(l_c, 16)
                        context(0, True)
                        queries_out(0, True)
                        keys_out(0, True)
                        act.wait_ge(l_ct, 16)
                        for c in range(NC):
                            nc.scalar.copy(Hh[:, c, :, 0, :], craw[:, c]).then_inc(a_ct, 1)

                        def body(j, first, last):
                            for n in range(NQ):
                                g = NQ * j + n
                                if not (first and n == 0):
                                    turned(g - 1)
                                powers(g)
                                if n == 0:
                                    if first:
                                        act.wait_ge(p_z, 3)
                                    values_out(j, first)
                                if n == 1:
                                    if not first:
                                        picked(j - 1)
                                    if not last:
                                        context(j + 1)
                                if n == 2 and not last:
                                    queries_out(j + 1)
                                if n == 3 and not last:
                                    keys_out(j + 1)

                        over_tiles(act, body)
                        turned(NQ * NT - 1)
                        picked(NT - 1)

                    @blk.vector
                    def _(dve):
                        dve_rows(dve, l_x)

                        def queries(j, first=False):
                            dve.wait_ge(a_q, j + 1)
                            if not first:
                                dve.wait_ge(s_s, NQ * j)
                            for h in range(HEADS0 // 2, HEADS0):
                                last = nc.vector.tensor_scalar(qx[:, :, h, :], qs[:].rearrange("p (n t) -> p n t", t=TB),
                                                               hmask[:, h:h + 1], None, ALU.mult)
                            last.then_inc(v_qx, 1)

                        def masked(g, start):
                            dve.wait_ge(s_av, g + 1)
                            if not start:
                                dve.wait_ge(s_sel, g)
                            nc.vector.tensor_tensor(
                                om[:].rearrange("p n b o -> p b n o"),
                                ps[:, AB:AB + 2, :].rearrange("p b (n o) -> p b n o", n=NB),
                                omask[:].unsqueeze(1).unsqueeze(1).broadcast_to((P, 2, NB, S)),
                                ALU.mult).then_inc(v_om, 1)

                        def add_output(j, own):
                            dve.wait_ge(s_wo, j + 1)
                            own(nc.vector.tensor_scalar(tmp[:], ps[:, PB, :], b0["o"][:], tg[:, 0:1], ALU.add, ALU.mult))
                            nc.vector.tensor_tensor(tile_of(x, j), tile_of(x, j), tmp[:], ALU.add).then_inc(v_x, 1)

                        bc = lambda y: y.unsqueeze(3).broadcast_to((P, 2, NB, KW))
                        per_tile = 3 * NQ + 1
                        queries(0, True)

                        def body(j, first, last):
                            own = Own(dve, v_own, 0 if first else per_tile * j - 1)
                            for n in range(NQ):
                                g = NQ * j + n
                                dve.wait_ge(s_s, g + 1)
                                own(nc.vector.tensor_tensor(sc[:], sv, band[:].unsqueeze(1).unsqueeze(1).broadcast_to(
                                    (P, 2, NB, KW)), ALU.add))
                                nc.vector.tensor_reduce(st[:, 0], sc[:], AX_X, ALU.max).then_inc(v_s, 1)
                                dve.wait_ge(v_s, g + 1)
                                nc.vector.tensor_tensor(sc[:], sc[:], bc(st[:, 0]), ALU.subtract).then_inc(v_sub, 1)
                                if n == 2 and not first:
                                    add_output(j - 1, own)
                                dve.wait_ge(a_e, g + 1)
                                own(nc.vector.tensor_reduce(st[:, 1], ex[:], AX_X, ALU.add))
                                own(nc.vector.reciprocal(st[:, 2], st[:, 1]))
                                if not (first and n == 0):
                                    dve.wait_ge(s_t, g)
                                nc.vector.tensor_tensor(pr[:], ex[:], bc(st[:, 2]), ALU.mult).then_inc(v_pr, 1)
                                if not (first and n == 0):
                                    masked(g - 1, first and n == 1)
                            if not last:
                                queries(j + 1)
                            assert own.n == per_tile - (1 if first else 0), own.n

                        over_tiles(dve, body)
                        masked(NQ * NT - 1, False)
                        add_output(NT - 1, Own(dve, v_own, per_tile * NT - 1))

        def phase_mixture(tag, gate, n_base, n_gate, wcat, wb, bias, store=None):
            l_w, a_w, p_w, v_w, s_ag, v_h, s_ht, a_ht, v_ht, s_y, v_own, v_z, a_z = (
                sem(f"m{tag}_{n}") for n in ("l_w", "a_w", "p_w", "v_w", "s_ag", "v_h", "s_ht", "a_ht", "v_ht", "s_y", "own",
                                             "v_z", "a_z"))
            l_wc = [sem(f"m{tag}_l_wc{c}") for c in range(NC)]
            v_x, l_out = sem(f"m{tag}_v_x"), sem(f"m{tag}_l_out")
            NW = n_base + P + n_gate
            RB = E8 * R16
            with ExitStack() as ph:
                xh = sb("mxh" + tag, [P, NC, TG], F32R, ctx=ph)
                xl = sb("mxl" + tag, [P, NC, TG], F32R, ctx=ph)
                dve_rows, pe_turn, act_high, dve_low, v_xn, v_xl, act_root = layer_norm("m" + tag, (xh, xl))
                wr = sb("mwr" + tag, [P, NC, NW], ctx=ph)
                wh = sb("mwh" + tag, [P, NC, NW], F32R, ctx=ph)
                wl = sb("mwl" + tag, [P, NC, NW], F32R, ctx=ph)
                br = sb("mbr" + tag, [P, D], ctx=ph)
                bh = sb("mbh" + tag, [P, D], F32R, ctx=ph)
                bl = sb("mbl" + tag, [P, D], F32R, ctx=ph)
                z = sb("mz" + tag, [P, NT, 16], ctx=ph)
                z2 = sb("mz2" + tag, [P, NT, 16], ctx=ph)
                m8 = sb("mm8" + tag, [P, NT, 8], ctx=ph)
                e = sb("me" + tag, [P, NT, E8], ctx=ph)
                w = sb("mw" + tag, [P, NT, E8], ctx=ph)
                s1 = sb("ms1" + tag, [P, 6, NT], ctx=ph)
                hp = sb("mhp" + tag, [P, NT, E8, R16], ctx=ph)
                th = sb("mth" + tag, [P, NT, P], F32R, ctx=ph)
                tl = sb("mtl" + tag, [P, NT, P], F32R, ctx=ph)
                with nc.Block() as blk:
                    @blk.sync
                    def _(sp):
                        for c in range(NC):
                            sp.dma_start(wr[:, c], wcat[:, c]).then_inc(l_wc[c], 16)
                        sp.dma_start(br[:], wb).then_inc(l_w, 16)
                        if store is not None:
                            for j in range(NT):
                                sp.wait_ge(v_x, j + 1)
                                sp.dma_start(store[:, j], x[:, j, :]).then_inc(l_out, 16)
                            sp.wait_ge(l_out, 16 * NT)

                    @blk.gpsimd
                    def _(pool):
                        for c in range(0, NC, 2):
                            pool.wait_ge(a_w, c + 1)
                            nc.gpsimd.tensor_tensor(wl[:, c], wr[:, c], f(wh[:, c]), ALU.subtract).then_inc(p_w, 1)
                        pool.wait_ge(a_w, NC + 1)
                        nc.gpsimd.tensor_tensor(bl[:], br[:], f(bh[:]), ALU.subtract).then_inc(p_w, 1)

                    @blk.scalar
                    def _(act):
                        act_root(act)
                        for j in range(NT):
                            act.wait_ge(l_wc[j], 16)
                            nc.scalar.copy(wh[:, j], wr[:, j]).then_inc(a_w, 1)
                            act_high(act, (j,))
                        act.wait_ge(l_w, 16)
                        nc.scalar.copy(bh[:], br[:]).then_inc(a_w, 1)
                        if gate == "threshold":
                            act.wait_ge(v_z, 1)
                            nc.scalar.activation(s1[:, 2, :], z[:, :, E8], ACT.Exp, bias=nbthr[:], scale=-1.0)
                        act.wait_ge(v_z, 1)
                        nc.scalar.activation(e[:], z2[:, :, 0:E8], ACT.Exp).then_inc(a_z, 1)
                        for j in range(NT):
                            act.wait_ge(s_ht, j + 1)
                            nc.scalar.copy(th[:, j, :], ps[:, j, 256:384]).then_inc(a_ht, 1)

                    @blk.tensor
                    def _(pe):
                        pe_turn(pe)
                        for j in range(NT):
                            pe.wait_ge(v_xl, j + 1)
                            rows = slice(j * P, (j + 1) * P)
                            for c in range(NC):
                                if j == 0:
                                    pe.wait_ge(v_w if c % 2 else p_w, c // 2 + 1)
                                last = passes(pe, ps[:, j, 0:P + n_gate], xh[:, c, rows], xl[:, c, rows],
                                              wh[:, c, n_base:NW], wl[:, c, n_base:NW], c == 0, c == NC - 1)
                            last.then_inc(s_ag, 1)

                        def dense(j):
                            if n_base:
                                rows = slice(j * P, (j + 1) * P)
                                nc.tensor.matmul(ps[:, 4 + j, :], ones[0:1, :], bias[:], start=True, stop=False)
                                for c in range(NC):
                                    passes(pe, ps[:, 4 + j, :], xh[:, c, rows], xl[:, c, rows],
                                           wh[:, c, 0:n_base], wl[:, c, 0:n_base], False, False)

                        def second(j):
                            pe.wait_ge(v_ht, j + 1)
                            passes(pe, ps[:, 4 + j, :], th[:, j, :], tl[:, j, :], bh[:], bl[:], not n_base,
                                   True).then_inc(s_y, 1)

                        dense(0)
                        dense(1)
                        for j in range(NT):
                            pe.wait_ge(v_h, j + 1)
                            nc.tensor.transpose(ps[:, j, 256:384], hp[:, j].rearrange("p e r -> p (e r)"),
                                                ident[:]).then_inc(s_ht, 1)
                        dense(2)
                        pe.wait_ge(p_w, NC // 2 + 1)
                        second(0)
                        second(1)
                        dense(3)
                        second(2)
                        second(3)

                    @blk.vector
                    def _(dve):
                        dve_rows(dve)
                        for j in range(NT):
                            if j % 2:
                                dve.wait_ge(a_w, j + 1)
                                nc.vector.tensor_tensor(wl[:, j], wr[:, j], f(wh[:, j]), ALU.subtract).then_inc(v_w, 1)
                            dve_low(dve, (j,))
                        own = Own(dve, v_own)
                        bc = lambda y: y.unsqueeze(2).broadcast_to((P, NT, E8))
                        logit = z[:, :, 0:E8]
                        dve.wait_ge(s_ag, NT)
                        own(nc.vector.memset(z[:], -BIG))
                        own(nc.vector.tensor_copy(z[:, :, 0:n_gate], ps[:, 0:NT, P:P + n_gate]))
                        if gate == "softmax":
                            own(nc.vector.tensor_tensor(logit, logit, br3[:].unsqueeze(1).broadcast_to((P, NT, E8)),
                                                        ALU.add))
                        own(nc.vector.tensor_reduce(s1[:, 0, :], logit, AX_X, ALU.max))
                        nc.vector.tensor_tensor(z2[:, :, 0:E8], logit, bc(s1[:, 0, :]), ALU.subtract).then_inc(v_z, 1)
                        if gate == "top2":
                            own(nc.vector.memset(m8[:], -BIG))
                            for j in range(NT):
                                own(nc.vector.max(w[:, j, :], z[:, j, 0:E8]))
                            own(nc.vector.tensor_copy(m8[:, :, 0:2], w[:, :, 0:2]))
                            dve.wait_ge(a_z, 1)
                            for j in range(NT):
                                own(nc.vector.match_replace(z2[:, j, :], m8[:, j, :], z[:, j, :], BIG))
                            own(nc.vector.tensor_tensor(w[:], z2[:, :, 0:E8], logit, ALU.not_equal))
                            own(nc.vector.tensor_tensor(e[:], e[:], w[:], ALU.mult))
                        dve.wait_ge(a_z, 1)
                        own(nc.vector.tensor_reduce(s1[:, 1, :], e[:], AX_X, ALU.add))
                        own(nc.vector.reciprocal(s1[:, 1, :], s1[:, 1, :]))
                        own(nc.vector.tensor_tensor(w[:], e[:], bc(s1[:, 1, :]), ALU.mult))
                        scale = LORA_SCALE
                        if gate == "threshold":
                            own(nc.vector.tensor_scalar(s1[:, 2, :], s1[:, 2, :], 1.0, None, ALU.add))
                            own(nc.vector.reciprocal(s1[:, 2, :], s1[:, 2, :]))
                            own(nc.vector.tensor_scalar(s1[:, 2, :], s1[:, 2, :], 1.0 / 8.0, None, ALU.mult))
                            own(nc.vector.tensor_tensor(w[:], w[:], bc(s1[:, 2, :]), ALU.subtract))
                            own(nc.vector.tensor_scalar(w[:], w[:], 0.0, None, ALU.max))
                            own(nc.vector.tensor_reduce(s1[:, 3, :], w[:], AX_X, ALU.add))
                            own(nc.vector.tensor_scalar(s1[:, 4, :], s1[:, 3, :], 0.0, None, ALU.is_equal))
                            own(nc.vector.tensor_tensor(s1[:, 3, :], s1[:, 3, :], s1[:, 4, :], ALU.add))
                            own(nc.vector.reciprocal(s1[:, 3, :], s1[:, 3, :]))
                            own(nc.vector.tensor_tensor(w[:], w[:], bc(s1[:, 3, :]), ALU.mult))
                        if gate == "softmax":
                            scale = LORA_SCALE * E8
                        own(nc.vector.tensor_scalar(w[:], w[:], scale, None, ALU.mult))
                        for j in range(NT):
                            nc.vector.tensor_tensor(hp[:, j], ps[:, j, 0:RB].rearrange("p (e r) -> p e r", e=E8),
                                                    w[:, j, :].unsqueeze(2).broadcast_to((P, E8, R16)),
                                                    ALU.mult).then_inc(v_h, 1)
                        for j in range(NT):
                            dve.wait_ge(a_ht, j + 1)
                            nc.vector.tensor_tensor(tl[:, j, :], ps[:, j, 256:384], f(th[:, j, :]),
                                                    ALU.subtract).then_inc(v_ht, 1)
                        for j in range(NT):
                            dve.wait_ge(s_y, j + 1)
                            nc.vector.scalar_tensor_tensor(out=x[:, j, :], in0=ps[:, 4 + j, :],
                                                           scalar=tg[:, 4 + int(tag):5 + int(tag)], in1=x[:, j, :],
                                                           op0=ALU.mult, op1=ALU.add).then_inc(v_x, 1)

        def phase_text():
            dve_rows, pe_turn, act_high, dve_low, v_xn, v_xl, act_root = layer_norm("t")
            l_w, a_w, p_w, s_p, a_p, v_p, s_s, v_m, a_e, v_pr, s_t, a_t, v_t, s_y, v_own, a_c, p_c = (
                sem("t_" + n) for n in ("l_w", "a_w", "p_w", "s_p", "a_p", "v_p", "s_s", "v_m", "a_e", "v_pr", "s_t",
                                        "a_t", "v_t", "s_y", "own", "a_c", "p_c"))
            SCALE = float(D) ** -0.5
            with ExitStack() as ph:
                wr = sb("twr", [P, 2, NC, D], ctx=ph)
                wh = sb("twh", [P, 2, NC, D], F32R, ctx=ph)
                wl = sb("twl", [P, 2, NC, D], F32R, ctx=ph)
                qh = sb("tqh", [P, 2, NC, TG], F32R, ctx=ph)
                ql = sb("tql", [P, 2, NC, TG], F32R, ctx=ph)
                cnh = sb("tch", [P, NT, D], F32R, ctx=ph)
                cnl = sb("tcl", [P, NT, D], F32R, ctx=ph)
                sc = sb("tsc", [P, NT, P], ctx=ph)
                ex = sb("tex", [P, NT, P], ctx=ph)
                st = sb("tst", [P, 3, NT], ctx=ph)
                th = sb("tth", [P, NT, P], F32R, ctx=ph)
                tl = sb("ttl", [P, NT, P], F32R, ctx=ph)
                bias = (bq2, bk2)
                with nc.Block() as blk:
                    @blk.sync
                    def _(sp):
                        sp.dma_start(wr[:, 1], a["L2_WkT"]).then_inc(l_w, 16)
                        sp.wait_ge(l_w, 16)
                        sp.dma_start(wr[:, 0], a["L2_WqT"]).then_inc(l_w, 16)

                    @blk.gpsimd
                    def _(pool):
                        for n, m in enumerate((1, 0)):
                            for c in range(NC):
                                pool.wait_ge(a_w, NC * n + c + 1)
                                nc.gpsimd.tensor_tensor(wl[:, m, c], wr[:, m, c], f(wh[:, m, c]),
                                                        ALU.subtract).then_inc(p_w, 1)
                        for j in range(NT):
                            pool.wait_ge(a_c, j + 1)
                            nc.gpsimd.tensor_tensor(cnl[:, j], cnat[:, j], f(cnh[:, j]), ALU.subtract).then_inc(p_c, 1)

                    @blk.scalar
                    def _(act):
                        act_root(act)
                        for n, m in enumerate((1, 0)):
                            act.wait_ge(l_w, 16 * (n + 1))
                            for c in range(NC):
                                nc.scalar.copy(wh[:, m, c], wr[:, m, c]).then_inc(a_w, 1)
                        act_high(act)
                        for n, m in enumerate((1, 0)):
                            for c in range(NC):
                                act.wait_ge(s_p, NC * n + c + 1)
                                nc.scalar.activation(qh[:, m, c], ps[:, 4 + c, :], ACT.Identity,
                                                     bias=bias[m][:, c:c + 1]).then_inc(a_p, 1)
                        for j in range(NT):
                            nc.scalar.copy(cnh[:, j], cnat[:, j]).then_inc(a_c, 1)
                        act.wait_ge(v_m, 1)
                        nc.scalar.activation(ex[:], sc[:], ACT.Exp, scale=SCALE).then_inc(a_e, 1)
                        act.wait_ge(s_t, 1)
                        nc.scalar.copy(th[:], ps[:, 1, :].rearrange("p (j k) -> p j k", j=NT)).then_inc(a_t, 1)

                    @blk.tensor
                    def _(pe):
                        def project(n, m, columns):
                            for e in columns:
                                if n:
                                    pe.wait_ge(v_p, e + 1)
                                for c in range(NC):
                                    pe.wait_ge(p_w, NC * n + c + 1)
                                    last = passes(pe, ps[:, 4 + e, :], wh[:, m, c, e * P:(e + 1) * P],
                                                  wl[:, m, c, e * P:(e + 1) * P], Hh[:, c, :, 1 - m, :],
                                                  Hl[:, c, :, 1 - m, :], c == 0, c == NC - 1)
                                last.then_inc(s_p, 1)
                        project(0, 1, range(NC // 2))
                        pe_turn(pe)
                        project(0, 1, range(NC // 2, NC))
                        pe.wait_ge(v_xl, NT)
                        project(1, 0, range(NC))
                        pe.wait_ge(v_p, 2 * NC)
                        for j in range(NT):
                            cols = slice(j * P, (j + 1) * P)
                            for c in range(NC):
                                last = passes(pe, ps[:, 0, cols], qh[:, 0, c, cols], ql[:, 0, c, cols],
                                              qh[:, 1, c, cols], ql[:, 1, c, cols], c == 0, c == NC - 1)
                        last.then_inc(s_s, 1)
                        pe.wait_ge(v_pr, 1)
                        for j in range(NT):
                            last = nc.tensor.transpose(ps[:, 1, j * P:(j + 1) * P], ex[:, j, :], ident[:])
                        last.then_inc(s_t, 1)
                        pe.wait_ge(v_t, 1)
                        pe.wait_ge(p_c, NT)
                        for j in range(NT):
                            passes(pe, ps[:, 4 + j, :], th[:, j, :], tl[:, j, :], cnh[:, j], cnl[:, j], True,
                                   True).then_inc(s_y, 1)

                    @blk.vector
                    def _(dve):
                        def low(n, m):
                            for e in range(NC):
                                dve.wait_ge(a_p, NC * n + e + 1)
                                nc.vector.scalar_tensor_tensor(out=ql[:, m, e], in0=ps[:, 4 + e, :],
                                                               scalar=bias[m][:, e:e + 1], in1=f(qh[:, m, e]),
                                                               op0=ALU.add, op1=ALU.subtract).then_inc(v_p, 1)
                        dve_rows(dve)
                        dve_low(dve)
                        low(0, 1)
                        low(1, 0)
                        own = Own(dve, v_own)
                        bc = lambda y: y.unsqueeze(2).broadcast_to((P, NT, P))
                        dve.wait_ge(s_s, 1)
                        own(nc.vector.tensor_tensor(sc[:], ps[:, 0, :].rearrange("p (j k) -> p j k", j=NT),
                                                    bmask[:].unsqueeze(1).broadcast_to((P, NT, P)), ALU.add))
                        own(nc.vector.tensor_reduce(st[:, 0], sc[:], AX_X, ALU.max))
                        nc.vector.tensor_tensor(sc[:], sc[:], bc(st[:, 0]), ALU.subtract).then_inc(v_m, 1)
                        dve.wait_ge(a_e, 1)
                        own(nc.vector.tensor_reduce(st[:, 1], ex[:], AX_X, ALU.add))
                        own(nc.vector.reciprocal(st[:, 2], st[:, 1]))
                        nc.vector.tensor_tensor(ex[:], ex[:], bc(st[:, 2]), ALU.mult).then_inc(v_pr, 1)
                        dve.wait_ge(a_t, 1)
                        nc.vector.tensor_tensor(tl[:], ps[:, 1, :].rearrange("p (j k) -> p j k", j=NT), f(th[:]),
                                                ALU.subtract).then_inc(v_t, 1)
                        for j in range(NT):
                            dve.wait_ge(s_y, j + 1)
                            nc.vector.scalar_tensor_tensor(out=x[:, j, :], in0=ps[:, 4 + j, :], scalar=tg[:, 2:3],
                                                           in1=x[:, j, :], op0=ALU.mult, op1=ALU.add)

        def context_values(tag, half, wv, vraw, ch, cl, ph):
            l_wv = [sem(f"{tag}_l_wv{c}") for c in range(NC)]
            a_wv, p_wv, a_c, p_c, s_v, a_v = (sem(f"{tag}_{n}") for n in ("a_wv", "p_wv", "a_c", "p_c", "s_v", "a_v"))
            HALF = 4 * HD
            rv = sb(f"{tag}_rv", [P, NC, HALF], ctx=ph)
            wvh, wvl = (sb(f"{tag}_{n}", [P, NC, HALF], F32R, ctx=ph) for n in ("wvh", "wvl"))

            def context(z, src, c, copy):
                return copy(z[:, c, :].rearrange("p (b t) -> p b t", t=S), f(src[:, c, :, 0, :]))

            def sp_load(sp):
                for c in range(NC):
                    sp.dma_start(rv[:, c], wv[:, c, half * HALF:(half + 1) * HALF]).then_inc(l_wv[c], 16)

            def act_context(act):
                for c in range(NC):
                    context(ch, Hh, c, nc.scalar.copy).then_inc(a_c, 1)

            def act_weights(act):
                for c in range(NC):
                    act.wait_ge(l_wv[c], 16)
                    nc.scalar.copy(wvh[:, c], rv[:, c]).then_inc(a_wv, 1)

            def act_out(act):
                for k in range(NT):
                    act.wait_ge(s_v, k + 1)
                    nc.scalar.copy(vraw[:, 4 * half:4 * half + 4, k, :],
                                   ps[:, 4 + k, :].rearrange("p (n d) -> p n d", d=HD)).then_inc(a_v, 1)

            def pool_low(pool):
                for c in range(NC):
                    if half == 0:
                        context(cl, Hl, c, nc.gpsimd.tensor_copy).then_inc(p_c, 1)
                    pool.wait_ge(a_wv, c + 1)
                    nc.gpsimd.tensor_tensor(wvl[:, c], rv[:, c], f(wvh[:, c]), ALU.subtract).then_inc(p_wv, 1)

            def pe_values(pe, tiles):
                for k in tiles:
                    for c in range(NC):
                        if k == 0:
                            pe.wait_ge(p_wv, c + 1)
                            if half == 0:
                                pe.wait_ge(a_c, c + 1)
                                pe.wait_ge(p_c, c + 1)
                        last = passes(pe, ps[:, 4 + k, :], ch[:, c, k * P:(k + 1) * P], cl[:, c, k * P:(k + 1) * P],
                                      wvh[:, c], wvl[:, c], c == 0, c == NC - 1)
                    last.then_inc(s_v, 1)

            return sp_load, act_context, act_weights, act_out, pool_low, pe_values, a_v

        def phase_ternary(values):
            dve_rows, _, _, _, v_xn, _, act_root = layer_norm("q")
            v_own, a_sq, v_q, s_t, a_t, s_y, v_y, a_g, v_ms, a_rr = (
                sem("q_" + n) for n in ("own", "a_sq", "v_q", "s_t", "a_t", "s_y", "v_y", "a_g", "v_ms",
                                         "a_rr"))
            with ExitStack() as ph:
                sq = sb("qsq", [P, NT, D], ctx=ph)
                rn = sb("qrn", [P, NT, D], ctx=ph)
                st = sb("qst", [P, 8, NT], ctx=ph)
                qi = sb("qi", [P, NT, D], BF16, ctx=ph)
                qt = sb("qt", [P, NC, TG], BF16, ctx=ph)
                y = sb("qy", [P, NT, D], ctx=ph)
                sp_load, act_context, act_weights, act_out, pool_low, pe_values, a_v = values(ph)
                with nc.Block() as blk:
                    @blk.sync
                    def _(sp):
                        sp_load(sp)

                    @blk.gpsimd
                    def _(pool):
                        pool_low(pool)

                    @blk.scalar
                    def _(act):
                        act_context(act)
                        act_root(act)
                        act_weights(act)
                        for j in range(NT):
                            act.wait_ge(v_xn, j + 1)
                            nc.scalar.activation(sq[:, j], xn[:, j], ACT.Square,
                                                 accum_out=st[:, 0, j:j + 1]).then_inc(a_sq, 1)
                        act.wait_ge(v_ms, 1)
                        root(act, st[:, 6], st[:, 1], a_rr, 0)
                        act_out(act)
                        for j in range(NT):
                            act.wait_ge(s_t, j + 1)
                            nc.scalar.copy(qt[:, :, j * P:(j + 1) * P],
                                           ps[:, j, 0:256].bitcast(BF16).rearrange("p (c t) -> p c t", c=NC)).then_inc(a_t, 1)
                        for j in range(NT):
                            act.wait_ge(v_y, j + 1)
                            nc.scalar.activation(sq[:, j], y[:, j], ACT.Gelu).then_inc(a_g, 1)
                        nc.scalar.preload_act_table_set(LN_EXP)

                    @blk.tensor
                    def _(pe):
                        pe_values(pe, range(NT))
                        for j in range(NT):
                            pe.wait_ge(v_q, j + 1)
                            dst = ps[:, j, 0:256].bitcast(BF16)
                            for c in range(NC):
                                last = nc.tensor.transpose(dst[:, c * P:(c + 1) * P], qi[:, j, c * P:(c + 1) * P],
                                                           identb[:])
                            last.then_inc(s_t, 1)
                        for j in range(NT):
                            pe.wait_ge(a_t, j + 1)
                            pe.wait_ge(a_v, j + 1)
                            for c in range(NC):
                                last = nc.tensor.matmul(ps[:, 4 + j, :], qt[:, c, j * P:(j + 1) * P], tern[:, c, :],
                                                        start=(c == 0), stop=(c == NC - 1))
                            last.then_inc(s_y, 1)

                    @blk.vector
                    def _(dve):
                        dve_rows(dve)
                        own = Own(dve, v_own)
                        dve.wait_ge(v_xn, NT)
                        nc.vector.tensor_reduce(st[:, 2], xn[:], AX_X, ALU.max)
                        dve.wait_ge(a_sq, NT)
                        nc.vector.tensor_scalar(st[:, 1], st[:, 0], 1.0 / D, EPS, ALU.mult, ALU.add).then_inc(v_ms, 1)
                        own(nc.vector.tensor_reduce(st[:, 3], xn[:], AX_X, ALU.min))
                        dve.wait_ge(a_rr, 2)
                        newton(own, st[:, 6], st[:, 1], st[:, 7])
                        for j in range(NT):
                            last = nc.vector.tensor_scalar(rn[:, j], xn[:, j], st[:, 6, j:j + 1], None, ALU.mult)
                        own(last)
                        own(nc.vector.tensor_scalar(st[:, 3], st[:, 3], -1.0, None, ALU.mult))
                        own(nc.vector.tensor_tensor(st[:, 2], st[:, 2], st[:, 3], ALU.max))
                        own(nc.vector.tensor_tensor(st[:, 2], st[:, 2], st[:, 6], ALU.mult))
                        own(nc.vector.tensor_scalar(st[:, 2], st[:, 2], EPS, None, ALU.max))
                        own(nc.vector.reciprocal(st[:, 4], st[:, 2]))
                        own(nc.vector.tensor_scalar(st[:, 4], st[:, 4], 127.0, None, ALU.mult))
                        own(nc.vector.tensor_scalar(st[:, 5], st[:, 2], wsc[:, 0:1], 1.0 / 127.0, ALU.mult, ALU.mult))
                        for j in range(NT):
                            last = nc.vector.tensor_scalar(rn[:, j], rn[:, j], st[:, 4, j:j + 1], None, ALU.mult)
                        own(last)
                        own(nc.vector.tensor_scalar(rn[:], rn[:], MAGIC, None, ALU.add))
                        own(nc.vector.tensor_scalar(rn[:], rn[:], MAGIC, 127.0, ALU.subtract, ALU.min))
                        for j in range(NT):
                            nc.vector.tensor_scalar(qi[:, j], rn[:, j], -128.0, None, ALU.max).then_inc(v_q, 1)
                        for j in range(NT):
                            dve.wait_ge(s_y, j + 1)
                            nc.vector.scalar_tensor_tensor(out=y[:, j], in0=ps[:, 4 + j, :], scalar=st[:, 5, j:j + 1],
                                                           in1=bf2[:], op0=ALU.mult, op1=ALU.add).then_inc(v_y, 1)
                        for j in range(NT):
                            dve.wait_ge(a_g, j + 1)
                            own(nc.vector.tensor_tensor(y[:, j], xn[:, j], sq[:, j], ALU.add))
                            nc.vector.scalar_tensor_tensor(out=x[:, j, :], in0=y[:, j], scalar=tg[:, 6:7],
                                                           in1=x[:, j, :], op0=ALU.mult, op1=ALU.add)

        def first_splits(tag):
            l_first = [sem(f"h{tag}_l_first{n}") for n in range(4)]
            a_first, p_first = sem(f"h{tag}_a_first"), sem(f"h{tag}_p_first")

            def sp_first(sp, raws):
                for n, (buf, src) in enumerate(raws):
                    sp.dma_start(buf, src).then_inc(l_first[n], 16)
                sp.wait_ge(l_first[3], 16)

            def act_first(act, splits):
                for n, (raw, high, _) in enumerate(splits):
                    act.wait_ge(l_first[n], 16)
                    nc.scalar.copy(high, raw).then_inc(a_first, 1)

            def pool_first(pool, splits):
                for n, (raw, high, low) in enumerate(splits):
                    pool.wait_ge(a_first, n + 1)
                    nc.gpsimd.tensor_tensor(low, raw, f(high), ALU.subtract).then_inc(p_first, 1)

            return sp_first, act_first, pool_first

        def phase_norm(values, first_loads, splits):
            dve_rows, pe_turn, act_high, dve_low, v_xn, v_xl, act_root = layer_norm("h3")
            sp_first, act_first, pool_first = first_splits("3")
            with ExitStack() as ph:
                sp_load, _, act_weights, act_out, pool_low, pe_values, _ = values(ph)
                with nc.Block() as blk:
                    @blk.sync
                    def _(sp):
                        sp_load(sp)
                        sp_first(sp, first_loads)

                    @blk.gpsimd
                    def _(pool):
                        pool_low(pool)
                        pool_first(pool, splits)

                    @blk.scalar
                    def _(act):
                        act_root(act)
                        act_weights(act)
                        act_first(act, splits)
                        act_high(act)
                        act_out(act)

                    @blk.tensor
                    def _(pe):
                        pe_values(pe, range(NT // 2))
                        pe_turn(pe)
                        pe_values(pe, range(NT // 2, NT))

                    @blk.vector
                    def _(dve):
                        dve_rows(dve)
                        dve_low(dve)

        def phase_values(tag, NKV, wv, vraw, first_loads, splits):
            dve_rows, pe_turn, act_high, dve_low, v_xn, v_xl, act_root = layer_norm("h" + tag)
            l_wv = [sem(f"h{tag}_l_wv{c}") for c in range(NC)]
            a_wv, p_wv, v_wv, s_v, a_v, v_v = (sem(f"h{tag}_{n}") for n in ("a_wv", "p_wv", "v_wv", "s_v", "a_v", "v_v"))
            sp_first, act_first, pool_first = first_splits(tag)
            assert NKV == 4
            with ExitStack() as ph:
                rv = sb("rv", [P, NC, NKV * HD], ctx=ph)
                wvh, wvl = (sb(n, [P, NC, NKV * HD], F32R, ctx=ph) for n in ("wvh", "wvl"))

                def bank(k):
                    return (k + 4) % 8

                def product(k):
                    return ps[:, bank(k), :].rearrange("p (n d) -> p n d", d=HD)

                with nc.Block() as blk:
                    @blk.sync
                    def _(sp):
                        for c in range(NC):
                            sp.dma_start(rv[:, c], wv[:, c]).then_inc(l_wv[c], 16)
                        sp_first(sp, first_loads)

                    @blk.gpsimd
                    def _(pool):
                        for c in range(0, NC, 2):
                            pool.wait_ge(a_wv, c + 1)
                            nc.gpsimd.tensor_tensor(wvl[:, c], rv[:, c], f(wvh[:, c]), ALU.subtract).then_inc(p_wv, 1)
                        pool_first(pool, splits)

                    @blk.scalar
                    def _(act):
                        def weights(c):
                            act.wait_ge(l_wv[c], 16)
                            nc.scalar.copy(wvh[:, c], rv[:, c]).then_inc(a_wv, 1)
                        weights(0)
                        weights(1)
                        act_root(act)
                        weights(2)
                        weights(3)
                        act_high(act)
                        act_first(act, splits)
                        for k in range(0, BG, 2):
                            act.wait_ge(s_v, k + 1)
                            nc.scalar.copy(vraw[:, :, k, :], product(k)).then_inc(a_v, 1)

                    @blk.tensor
                    def _(pe):
                        pe_turn(pe)
                        for k in range(BG):
                            pe.wait_ge(v_xl, max(k // 2 + 1, k - 3))
                            for c in range(NC):
                                if k == 0:
                                    pe.wait_ge(v_wv if c % 2 else p_wv, c // 2 + 1)
                                last = passes(pe, ps[:, bank(k), :], Hh[:, c, k].rearrange("p s t -> p (s t)"),
                                              Hl[:, c, k].rearrange("p s t -> p (s t)"), wvh[:, c], wvl[:, c], c == 0, c == NC - 1)
                            last.then_inc(s_v, 1)

                    @blk.vector
                    def _(dve):
                        dve_rows(dve)
                        for c in range(1, NC, 2):
                            dve.wait_ge(a_wv, c + 1)
                            nc.vector.tensor_tensor(wvl[:, c], rv[:, c], f(wvh[:, c]), ALU.subtract).then_inc(v_wv, 1)
                        dve_low(dve)
                        for k in range(1, BG, 2):
                            dve.wait_ge(s_v, k + 1)
                            nc.vector.tensor_copy(vraw[:, :, k, :], product(k)).then_inc(v_v, 1)

        def phase_heads(tag, NKV, HP, KEYS, norm, wq, wo, wk, wv, gate):
            with ExitStack() as ph:
                vraw = sb(f"h{tag}_vraw", [P, NKV, NT if norm else BG, HD], ctx=ph)
                rq, ro, rk = (sb(f"h{tag}_{n}", shape, ctx=ph) for n, shape in (
                    ("rq", [P, 2, NC, 2 * HD]), ("ro", [P, 2, 2, D]), ("rk", [P, NC, HD])))
                wqh, wql = (sb(f"h{tag}_{n}", [P, 2, NC, 2 * HD], F32R, ctx=ph) for n in ("wqh", "wql"))
                wkh, wkl = (sb(f"h{tag}_{n}", [P, NC, HD], F32R, ctx=ph) for n in ("wkh", "wkl"))
                splits = ((rk[:], wkh[:], wkl[:]), (rq[:, 0], wqh[:, 0], wql[:, 0]), (rq[:, 1], wqh[:, 1], wql[:, 1]))
                raw = lambda buf, src, n: (buf.rearrange("p c n -> p (c n)"), src[n])
                first_loads = (raw(rk[:], wk, 0), raw(rq[:, 0], wq, 0), raw(rq[:, 1], wq, 1), raw(ro[:, 0], wo, 0))
                if norm:
                    with ExitStack() as ctx:
                        ch, cl = (sb(n, [P, NC, TG], F32R, ctx=ctx) for n in ("ch", "cl"))
                        phase_ternary(lambda ph: context_values("v0", 0, wv, vraw, ch, cl, ph))
                        end_phase()
                        phase_norm(lambda ph: context_values("v1", 1, wv, vraw, ch, cl, ph), first_loads, splits)
                        end_phase()
                else:
                    phase_values(tag, NKV, wv, vraw, first_loads, splits)
                    end_phase()
                heads(tag, NKV, HP, KEYS, norm, wq, wo, wk, vraw, rq, ro, rk, wqh, wql, wkh, wkl, gate)

        def heads(tag, NKV, HP, KEYS, norm, wq, wo, wk, vraw, rq, ro, rk, wqh, wql, wkh, wkl, gate):
            NS = 2 * HP
            NSTEP = NKV * NS
            NP = NKV * HP
            HB = BG // 2
            SCALE = float(HD) ** -0.5
            names = ("s_q", "a_q", "v_q", "s_k", "a_ksq", "s_kss", "s_qss", "v_kn", "a_kn", "a_k", "v_k", "a_v", "v_v", "s_s",
                     "v_s", "v_m", "a_e", "v_p", "s_t", "a_t", "v_t", "s_av", "a_o", "v_o", "s_wo", "a_wq", "p_wq",
                     "a_wo", "p_wo", "a_kv", "p_kv", "l_kv", "v_own", "a_krs", "a_qrs", "p_z", "lq0", "lq1", "lo0", "lo1")
            m = {n: sem(f"h{tag}_{n}") for n in names}
            QB, SBK, TBK, AB, OB = 0, 1, 2, 3, 4
            PT = 128 * (HB * KEYS // P)
            EQ = 32
            with ExitStack() as ph:
                def tb(name, shape, dt=F32):
                    return sb(f"h{tag}_{name}", shape, dt, ctx=ph)
                woh, wol = tb("woh", [P, 2, 2, D], F32R), tb("wol", [P, 2, 2, D], F32R)
                qh, ql = tb("qh", [P, 2, BG, 2, S], F32R), tb("ql", [P, 2, BG, 2, S], F32R)
                kh, kl = tb("kh", [P, BG, KEYS], F32R), tb("kl", [P, BG, KEYS], F32R)
                vh, vl = tb("vh", [P, BG, HD], F32R), tb("vl", [P, BG, HD], F32R)
                kn = tb("kn", [P, BG, KEYS])
                ex, pr = tb("ex", [P, HB, KEYS]), tb("pr", [P, HB, KEYS])
                mx = tb("mx", [P, 6, HB])
                th, tl = tb("th", [P, PT], F32R), tb("tl", [P, PT], F32R)
                oh, ol = tb("oh", [P, 2, HB, S], F32R), tb("ol", [P, 2, HB, S], F32R)
                if norm:
                    sq, ksq, rks, sc = (tb("sq", [P, 2, BG, 2, S]), tb("ksq", [P, TG]), tb("rks", [P, TG]),
                                        tb("sc", [P, HB, KEYS]))
                    qrs = tb("qrs", [P, 2, BG])

                def values_raw(i, r):
                    return vraw[r, bass.ds(i, 1)].rearrange("p a j d -> p (a j) d")

                def ring_of(z, n):
                    return z[:, n // 2, :, n % 2, :]

                def by_batch(bank):
                    return ps[:, bank, :].rearrange("p (b t) -> p b t", t=S)

                def by_head(z):
                    return z[:].rearrange("p h b t -> p b h t")

                def kbank(bank):
                    return ps[:, bank, :].rearrange("p (b k) -> p b k", k=KEYS)

                with nc.Block() as blk:
                    def split_steps(eng, i, t, last, kv, q, o):
                        if t == 1 and not last:
                            kv(i + 1)
                        if t % 2:
                            mm = (t - 1) // 2
                            if not (last and mm + 2 >= HP):
                                q(i * HP + mm + 2, mm % 2, i * (HP // 2) + (mm + 2) // 2)
                            if not (last and mm + 1 >= HP):
                                o(i * HP + mm + 1, (mm + 1) % 2, i * (HP // 2) + (mm + 1) // 2)

                    def over_groups(eng, body):
                        body(0, True, False)
                        with eng.Fori(1, NKV - 1) as i:
                            body(i, False, False)
                        body(NKV - 1, False, True)

                    @blk.sync
                    def _(sp):
                        def load_kv(i):
                            wait(sp, m["p_kv"], i - 1)
                            sp.dma_start(rk[:].rearrange("p c n -> p (c n)"),
                                         wk[bass.ds(i, 1)].rearrange("i p n -> (i p) n")).then_inc(m["l_kv"], 16)

                        def load(n, par, split, before, signal, buf, src):
                            wait(sp, m[split], n - 1 - before)
                            sp.dma_start(buf[:, par].rearrange("p c n -> p (c n)"),
                                         src[bass.ds(n, 1)].rearrange("i p n -> (i p) n")).then_inc(m[f"{signal}{par}"], 16)

                        def load_q(n, par, _=0):
                            load(n, par, "p_wq", 2, "lq", rq, wq)

                        def load_o(n, par, _=0):
                            load(n, par, "p_wo", 0, "lo", ro, wo)

                        def body(i, first, last):
                            for t in range(NS):
                                split_steps(sp, i, t, last, load_kv, load_q, load_o)
                        over_groups(sp, body)

                    @blk.gpsimd
                    def _(pool):
                        if norm:
                            nc.gpsimd.memset(f(vh[:]), 0.0).then_inc(m["p_z"], 1)
                            nc.gpsimd.memset(f(vl[:]), 0.0).then_inc(m["p_z"], 1)

                        def kv(i):
                            pool.wait_ge(m["a_kv"], i)
                            nc.gpsimd.tensor_tensor(wkl[:], rk[:], f(wkh[:]), ALU.subtract).then_inc(m["p_kv"], 1)

                        def q(n, par, _):
                            pool.wait_ge(m["a_wq"], n - 1)
                            nc.gpsimd.tensor_tensor(wql[:, par], rq[:, par], f(wqh[:, par]), ALU.subtract).then_inc(m["p_wq"], 1)

                        def o(n, par, _):
                            pool.wait_ge(m["a_wo"], n + 1)
                            nc.gpsimd.tensor_tensor(wol[:, par], ro[:, par], f(woh[:, par]), ALU.subtract).then_inc(m["p_wo"], 1)
                        o(0, 0, 0)

                        def body(i, first, last):
                            for t in range(NS):
                                split_steps(pool, i, t, last, kv, q, o)
                        over_groups(pool, body)

                    @blk.scalar
                    def _(act):
                        def kv(i):
                            wait(act, m["l_kv"], 16 * i)
                            wait(act, m["s_k"], i if norm else 2 * i)
                            nc.scalar.copy(wkh[:], rk[:]).then_inc(m["a_kv"], 1)

                        def q(n, par, u):
                            wait(act, m[f"lq{par}"], 16 * u)
                            wait(act, m["s_q"], 2 * n - 2)
                            nc.scalar.copy(wqh[:, par], rq[:, par]).then_inc(m["a_wq"], 1)

                        def o(n, par, u):
                            wait(act, m[f"lo{par}"], 16 * (u + par))
                            wait(act, m["s_wo"], 2 * n - 2)
                            nc.scalar.copy(woh[:, par], ro[:, par]).then_inc(m["a_wo"], 1)

                        def keys_out(i):
                            if type(i) is not int or i > 0:
                                act.wait_ge(m["v_k"], i)
                            for half, bank in enumerate((QB, TBK)):
                                act.wait_ge(m["s_k"], 2 * i + half + 1)
                                nc.scalar.copy(kn[:, HB * half:HB * half + HB], kbank(bank)).then_inc(m["a_kn"], 1)

                        def keys_high(i, n):
                            if norm:
                                act.wait_ge(m["v_kn"], i + 1)
                            else:
                                act.wait_ge(m["a_kn"], 2 * i + 2)
                            wait(act, m["s_s"], n)
                            nc.scalar.copy(kh[:], kn[:]).then_inc(m["a_k"], 1)

                        def keys_root(i):
                            act.wait_ge(m["s_kss"], i + 1)
                            root(act, rks[:], ps[:, AB, :], m["a_krs"], 2 * i, 1.0 / HD, EPS)

                        def queries_root(k, pair):
                            act.wait_ge(m["s_qss"], k + 1)
                            root(act, qrs[:, pair], ps[:, SBK, HB * KEYS:2 * HB * KEYS].rearrange("p (b e) -> p b e", e=EQ)[:, :, 0],
                                 m["a_qrs"], 2 * k, 1.0 / HD, EPS, math.log(SCALE))

                        def keys_square(i):
                            act.wait_ge(m["s_k"], i + 1)
                            nc.scalar.activation(ksq[:], ps[:, TBK, :], ACT.Square).then_inc(m["a_ksq"], 1)

                        def head_high(n, ring):
                            act.wait_ge(m["s_q"], n + 1)
                            if norm:
                                nc.scalar.activation(ring_of(sq, ring), by_batch(QB), ACT.Square)
                            nc.scalar.copy(ring_of(qh, ring), by_batch(QB)).then_inc(m["a_q"], 1)

                        def turned_high(n):
                            act.wait_ge(m["s_t"], n)
                            nc.scalar.copy(th[:], ps[:, TBK, 0:PT]).then_inc(m["a_t"], 1)

                        def out_high(n):
                            act.wait_ge(m["s_av"], n)
                            nc.scalar.copy(by_head(oh), ps[:, AB, :].rearrange("p (b h t) -> p b h t", h=2, t=S)).then_inc(m["a_o"], 1)

                        o(0, 0, 0)
                        if norm:
                            keys_square(0)
                        else:
                            keys_out(0)
                        head_high(0, 0)
                        if norm:
                            keys_root(0)
                        keys_high(0, 0)
                        head_high(1, 1)
                        if norm:
                            queries_root(0, 0)

                        def body(i, first, last):
                            for t in range(NS):
                                n = i * NS + t
                                act.wait_ge(m["v_m"], n + 1)
                                if not (first and t == 0):
                                    act.wait_ge(m["v_p"], n)
                                if norm:
                                    nc.scalar.activation(ex[:], sc[:], ACT.Exp).then_inc(m["a_e"], 1)
                                else:
                                    for b in range(HB):
                                        ins = nc.scalar.activation(ex[:, b], kbank(SBK)[:, b], ACT.Exp, bias=mx[:, 1, b:b + 1],
                                                                   scale=SCALE, accum_out=mx[:, 2, b:b + 1])
                                    ins.then_inc(m["a_e"], 1)
                                if t == NS - 2 and not last:
                                    if norm:
                                        keys_square(i + 1)
                                    else:
                                        keys_out(i + 1)
                                if t == NS - 1 and not last:
                                    keys_high(i + 1, n + 1)
                                if not (last and t >= NS - 2):
                                    head_high(n + 2, (t + 2) % 4)
                                if norm and t == NS - 2 and not last:
                                    keys_root(i + 1)
                                if not (first and t == 0):
                                    turned_high(n)
                                split_steps(act, i, t, last, kv, q, o)
                                if norm and t % 2 and not (last and t == NS - 1):
                                    queries_root(i * HP + (t + 1) // 2, (t + 1) // 2 % 2)
                                if not (first and t == 0):
                                    out_high(n)
                                if t == 0:
                                    if norm:
                                        if first:
                                            act.wait_ge(m["p_z"], 2)
                                        for b in range(2):
                                            r = slice(64 * b, 64 * b + 64)
                                            ins = nc.scalar.copy(vh[r, b::2, :], values_raw(i, r))
                                    else:
                                        ins = nc.scalar.copy(vh[:], values_raw(i, slice(0, P)))
                                    ins.then_inc(m["a_v"], 1)
                        over_groups(act, body)
                        turned_high(NSTEP)
                        out_high(NSTEP)

                    @blk.tensor
                    def _(pe):
                        for j in range(NT):
                            nc.tensor.matmul(ps[:, OB + j, :], zb[:, 0:P], zb[:], start=True, stop=False,
                                             skip_group_check=True)

                        def keys(i):
                            wait(pe, m["p_kv"], i)
                            for half in range(1 if norm else 2):
                                if half:
                                    last.then_inc(m["s_k"], 1)
                                for c in range(NC):
                                    rhs = [(X[:, c, :, 0, :] if norm else
                                            X[:, c, HB * half:HB * half + HB].rearrange("p b s t -> p (b s t)")) for X in (Hh, Hl)]
                                    last = passes(pe, ps[:, TBK if norm or half else QB, :], wkh[:, c], wkl[:, c],
                                                  rhs[0], rhs[1], c == 0, c == NC - 1)
                            last.then_inc(m["s_k"], 1)

                        def keys_sum(i):
                            pe.wait_ge(m["a_ksq"], i + 1)
                            nc.tensor.matmul(ps[:, AB, :], ones[:], ksq[:], start=True, stop=True).then_inc(m["s_kss"], 1)

                        def head(n, hh, ring, par):
                            for c in range(NC):
                                last = passes(pe, ps[:, QB, :], wqh[:, par, c, hh * HD:(hh + 1) * HD],
                                              wql[:, par, c, hh * HD:(hh + 1) * HD], Hh[:, c, :, 1, :], Hl[:, c, :, 1, :],
                                              c == 0, c == NC - 1)
                            last.then_inc(m["s_q"], 1)

                        def scores(t):
                            pair = (t // 2) % 2
                            for b4 in range(HB):
                                b = HB * (t % 2) + b4
                                mine = lambda z: z[:, pair, b].rearrange("p h t -> p (h t)")
                                last = passes(pe, ps[:, SBK, b4 * KEYS:(b4 + 1) * KEYS], mine(qh), mine(ql), kh[:, b], kl[:, b],
                                              True, True)
                            last.then_inc(m["s_s"], 1)

                        def squares_sum(n, pair):
                            pe.wait_ge(m["a_q"], n + 2)
                            for b in range(BG):
                                col = HB * KEYS + EQ * b
                                last = nc.tensor.matmul(ps[:, SBK, col:col + EQ], sq[:, pair, b].rearrange("p h t -> p (h t)"),
                                                        ones[:, 0:EQ], start=True, stop=True)
                            last.then_inc(m["s_qss"], 1)

                        def turn():
                            for c in range(PT // P):
                                last = nc.tensor.transpose(ps[:, TBK, c * P:(c + 1) * P],
                                                           pr[:].rearrange("p b k -> p (b k)")[:, c * P:(c + 1) * P], ident[:])
                            last.then_inc(m["s_t"], 1)

                        def values_of(t):
                            for b4 in range(HB):
                                b = HB * (t % 2) + b4
                                c = b4 * KEYS // P
                                last = passes(pe, ps[:, AB, b4 * P:(b4 + 1) * P], vh[:, b], vl[:, b], th[:, c * P:(c + 1) * P],
                                              tl[:, c * P:(c + 1) * P], True, True)
                            last.then_inc(m["s_av"], 1)

                        def output(t, final=False):
                            par = (t // 2) % 2
                            for jj in range(2):
                                for h in range(2):
                                    last = passes(pe, ps[:, OB + 2 * (t % 2) + jj, :], oh[:, h, 2 * jj:2 * jj + 2].rearrange("p b t -> p (b t)"),
                                                  ol[:, h, 2 * jj:2 * jj + 2].rearrange("p b t -> p (b t)"), woh[:, par, h], wol[:, par, h], False,
                                                  final and h == 1, skip_group_check=True)
                            last.then_inc(m["s_wo"], 1)

                        keys(0)
                        if not norm:
                            pe.wait_ge(m["a_kn"], 1)
                        head(0, 0, 0, 0)
                        if norm:
                            keys_sum(0)
                        pe.wait_ge(m["v_q"], 1)
                        head(1, 1, 1, 0)
                        if norm:
                            squares_sum(0, 0)

                        def body(i, first, last):
                            for t in range(NS):
                                n = i * NS + t
                                start = first and t == 0
                                if t % 2 == 0:
                                    pe.wait_ge(m["v_q"], n + 2)
                                if t == 0:
                                    pe.wait_ge(m["v_k"], i + 1)
                                if not start:
                                    pe.wait_ge(m["v_s" if norm else "a_e"], n)
                                if norm and t % 2 == 0:
                                    pe.wait_ge(m["a_qrs"], 2 * (i * HP + t // 2) + 1)
                                scores(t)
                                if t == NS - 2 and not last:
                                    pe.wait_ge(m["v_q"], n + 2)
                                    pe.wait_ge(m["v_t"], n - 1)
                                    keys(i + 1)
                                    if not norm:
                                        pe.wait_ge(m["a_kn"], 2 * i + 3)
                                if not (last and t >= NS - 2):
                                    pe.wait_ge(m["v_q"], n + 2)
                                    if t % 2 == 0:
                                        wait(pe, m["p_wq"], i * HP + t // 2)
                                    head(n + 2, t % 2, (t + 2) % 4, ((t + 2) // 2) % 2)
                                if t == NS - 2 and not last:
                                    if norm:
                                        pe.wait_ge(m["v_o"], n - 1)
                                        keys_sum(i + 1)
                                    else:
                                        pe.wait_ge(m["a_kn"], 2 * i + 4)

                                def product():
                                    pe.wait_ge(m["v_o"], n - 1)
                                    if t % 2 == 0:
                                        pe.wait_ge(m["p_wo"], i * HP + t // 2)
                                    output((t - 2) % NS)
                                early = norm and t == NS - 2 and not last and not (first and t < 2)
                                if early:
                                    product()
                                    pe.wait_ge(m["v_kn"], i + 2)
                                if not start:
                                    pe.wait_ge(m["v_p"], n)
                                    if not (first and t == 1):
                                        pe.wait_ge(m["v_t"], n - 1)
                                    turn()
                                if not (first and t < 2) and not early:
                                    product()
                                if norm and t % 2 and not (last and t == NS - 1):
                                    pe.wait_ge(m["v_s"], n + 1)
                                    squares_sum(n + 1, (t + 1) // 2 % 2)
                                if not start:
                                    pe.wait_ge(m["v_t"], n)
                                    if t == 1:
                                        pe.wait_ge(m["v_v"], i + 1)
                                    values_of((t - 1) % NS)
                        over_groups(pe, body)
                        pe.wait_ge(m["v_p"], NSTEP)
                        pe.wait_ge(m["v_t"], NSTEP - 1)
                        turn()
                        pe.wait_ge(m["v_o"], NSTEP - 1)
                        pe.wait_ge(m["p_wo"], NP)
                        output(NS - 2, True)
                        pe.wait_ge(m["v_t"], NSTEP)
                        values_of(NS - 1)
                        pe.wait_ge(m["v_o"], NSTEP)
                        output(NS - 1, True)

                    @blk.vector
                    def _(dve):
                        def keys_norm(i):
                            dve.wait_ge(m["a_krs"], 2 * i + 2)
                            if type(i) is not int or i > 0:
                                dve.wait_ge(m["v_k"], i)
                            nc.vector.scalar_tensor_tensor(out=kn[:].rearrange("p b k -> p (b k)"), in0=ps[:, TBK, :], scalar=qkw[:], in1=rks[:],
                                                           op0=ALU.mult, op1=ALU.mult).then_inc(m["v_kn"], 1)

                        def keys_low(i):
                            dve.wait_ge(m["a_k"], i + 1)
                            nc.vector.tensor_tensor(kl[:], kn[:], f(kh[:]), ALU.subtract).then_inc(m["v_k"], 1)

                        def head_low(n, ring):
                            dve.wait_ge(m["a_q"], n + 1)
                            nc.vector.tensor_tensor(ring_of(ql, ring), by_batch(QB), f(ring_of(qh, ring)), ALU.subtract).then_inc(m["v_q"], 1)

                        def turned_low(n):
                            dve.wait_ge(m["a_t"], n)
                            nc.vector.tensor_tensor(tl[:], ps[:, TBK, 0:PT], f(th[:]), ALU.subtract).then_inc(m["v_t"], 1)

                        def out_low(n):
                            dve.wait_ge(m["a_o"], n)
                            nc.vector.tensor_tensor(by_head(ol), ps[:, AB, :].rearrange("p (b h t) -> p b h t", h=2, t=S),
                                                    f(by_head(oh)), ALU.subtract).then_inc(m["v_o"], 1)

                        bc = lambda y: y.unsqueeze(2).broadcast_to((P, HB, KEYS))

                        def largest(i, t, own):
                            n = i * NS + t
                            dve.wait_ge(m["s_s"], n + 1)
                            if norm:
                                dve.wait_ge(m["a_qrs"], 2 * (i * HP + t // 2) + 2)
                                half = slice(HB * (t % 2), HB * (t % 2) + HB)
                                nc.vector.tensor_tensor(sc[:], kbank(SBK)[:, 0:HB], bc(qrs[:, t // 2 % 2, half]), ALU.mult).then_inc(m["v_s"], 1)
                                dve.wait_ge(m["v_s"], n + 1)
                                own(nc.vector.tensor_tensor(sc[:], sc[:], mask3[:].unsqueeze(1).broadcast_to((P, HB, KEYS)), ALU.add))
                                own(nc.vector.tensor_reduce(mx[:, 0], sc[:], AX_X, ALU.max))
                                nc.vector.tensor_tensor(sc[:], sc[:], bc(mx[:, 0]), ALU.subtract).then_inc(m["v_m"], 1)
                            else:
                                own(nc.vector.tensor_reduce(mx[:, 0], kbank(SBK), AX_X, ALU.max))
                                nc.vector.tensor_scalar(mx[:, 1], mx[:, 0], -SCALE, None, ALU.mult).then_inc(m["v_m"], 1)

                        def shares(n, own, start):
                            dve.wait_ge(m["a_e"], n + 1)
                            if norm:
                                own(nc.vector.tensor_reduce(mx[:, 2], ex[:], AX_X, ALU.add))
                            own(nc.vector.reciprocal(mx[:, 5], mx[:, 2]))
                            if not start:
                                dve.wait_ge(m["s_t"], n)
                            nc.vector.tensor_tensor(pr[:], ex[:], bc(mx[:, 5]), ALU.mult).then_inc(m["v_p"], 1)

                        head_low(0, 0)
                        if norm:
                            keys_norm(0)
                        keys_low(0)
                        head_low(1, 1)
                        per_step = 4 if norm else 2

                        def body(i, first, last):
                            own = Own(dve, m["v_own"], per_step * NS * i)
                            for t in range(NS):
                                n = i * NS + t
                                start = first and t == 0
                                largest(i, t, own)
                                if t == NS - 1 and not last:
                                    keys_low(i + 1)
                                if not (last and t >= NS - 2):
                                    head_low(n + 2, (t + 2) % 4)
                                if t == NS - 2 and not last and norm:
                                    keys_norm(i + 1)
                                if not start:
                                    turned_low(n)
                                shares(n, own, start)
                                if not start:
                                    out_low(n)
                                if t == 0:
                                    dve.wait_ge(m["a_v"], i + 1)
                                    if norm:
                                        for b in range(2):
                                            r = slice(64 * b, 64 * b + 64)
                                            ins = nc.vector.tensor_tensor(vl[r, b::2, :], values_raw(i, r), f(vh[r, b::2, :]), ALU.subtract)
                                    else:
                                        ins = nc.vector.tensor_tensor(vl[:], values_raw(i, slice(0, P)), f(vh[:]), ALU.subtract)
                                    ins.then_inc(m["v_v"], 1)
                            assert own.n == per_step * NS, own.n
                        over_groups(dve, body)
                        turned_low(NSTEP)
                        out_low(NSTEP)
                        dve.wait_ge(m["s_wo"], NSTEP)
                        for j in range(NT):
                            nc.vector.scalar_tensor_tensor(out=x[:, j, :], in0=ps[:, OB + j, :], scalar=tg[:, gate:gate + 1],
                                                           in1=x[:, j, :], op0=ALU.mult, op1=ALU.add)

        end_phase()
        with nc.Fori(0, groups) as g:
            for phase in (
                    lambda: phase_local(g),
                    lambda: phase_mixture("0", "top2", D, E8, a["L0_wcat"], a["L0_B"], bbase["0"]),
                    lambda: phase_heads("1", 4, 4, 2 * S, False, a["L1_Wq"], a["L1_Wo"], a["L1_Wk"], a["L1_Wv"], 1),
                    lambda: phase_mixture("1", "threshold", D, E8 + 2, a["L1_wcat"], a["L1_B"], bbase["1"]),
                    phase_text,
                    lambda: phase_heads("3", 8, 2, S, True, a["L3_Wq"], a["L3_Wo"], a["L3_Wk"], a["L3_Wv"], 3),
                    lambda: phase_mixture("3", "softmax", 0, E8, a["L3_wcat"], a["L3_B"], None,
                                          out[bass.ds(g, 1)].rearrange("a p t d -> (a p) t d"))):
                phase()
                end_phase()


def constants():
    r = np.arange(P)
    head, query = r // TB, r % TB
    key = np.arange(KW)
    gap = key[None, :] - query[:, None]
    v = np.zeros((8, 4, KW), np.float32)
    for q in range(8):
        for t in range(4):
            pos = (4 * q + t) * TB - WIN // 2 + key
            v[q, t] = (pos >= 0) & (pos < D)
    return {
        "c_ident": np.eye(P, dtype=np.float32),
        "c_hmask": ((r[:, None] % S) // HD0 == np.arange(HEADS0)[None, :]).astype(np.float32),
        "c_band": np.where((gap >= 0) & (gap < WIN), 0.0, -1e30).astype(np.float32),
        "c_omask": (np.arange(S)[None, :] // HD0 == head[:, None]).astype(np.float32),
        "c_osel": (query[:, None] == np.arange(TB)[None, :]).astype(np.float32),
        "c_bmask": np.where(r[:, None] // S == r[None, :] // S, 0.0, -1e30).astype(np.float32),
        "c_vrow": v.reshape(1, 8 * P),
    }


def layouts(i):
    def rows(z):
        return z.reshape(G, NT, P, D).transpose(0, 2, 1, 3)

    def chunks(z):
        return z.reshape(NC, P, -1).transpose(1, 0, 2)

    def pairs_in(z):
        return z.reshape(NC, P, -1, 2 * HD).transpose(2, 1, 0, 3).reshape(-1, P, NC * 2 * HD)

    def pairs_out(z):
        return z.reshape(-1, 2, HD, D).transpose(0, 2, 1, 3).reshape(-1, P, 2 * D)

    def keys(k):
        return k.reshape(NC, P, -1, HD).transpose(2, 1, 0, 3).reshape(-1, P, NC * HD)

    def second(z):
        return z.transpose(0, 2, 1).reshape(E8 * R16, D)

    def first(*parts):
        return chunks(np.concatenate([p.reshape(-1, D).T for p in parts], axis=1))

    d = {
        "x": rows(i["x"]), "ctx": rows(i["ctx_4096"]),
        "ctxT": i["ctx_4096"].reshape(G, TG, NC, P).transpose(0, 3, 2, 1),
        "mask": i["mask_1x1xSxS2_ff0"].reshape(S, S),
        "g_xattn": i["g_xattn"], "g_ffn": i["g_ffn"],
        "L0_wcat": first(i["L0_ffn_W_base"], i["L0_ffn_A"], i["L0_ffn_W_router"]),
        "L0_B": second(i["L0_ffn_B"]),
        "L1_Wq": pairs_in(i["L1_xattn_Wq"]), "L1_Wo": pairs_out(i["L1_xattn_Wo"]),
        "L1_Wk": keys(i["L1_xattn_Wk"]), "L1_Wv": chunks(i["L1_xattn_Wv"]),
        "L1_wcat": first(i["L1_ffn_W_base"], i["L1_ffn_A"], i["L1_ffn_W_gate"], i["L1_ffn_W_thr"], i["L1_ffn_W_thr"]),
        "L1_B": second(i["L1_ffn_B"]),
        "L2_WqT": chunks(i["L2_xattn_Wq"].T), "L2_WkT": chunks(i["L2_xattn_Wk"].T),
        "L2_bq": i["L2_xattn_bq"].reshape(NC, P).T, "L2_bk": i["L2_xattn_bk"].reshape(NC, P).T,
        "L2_ffn_WT": chunks(i["L2_ffn_W"].T),
        "L3_Wq": pairs_in(i["L3_xattn_Wq"].T), "L3_Wo": pairs_out(i["L3_xattn_Wo"].T),
        "L3_Wk": keys(i["L3_xattn_Wk"].T), "L3_Wv": chunks(i["L3_xattn_Wv"].T),
        "L3_wcat": first(i["L3_ffn_A"], i["L3_ffn_Wr"]),
        "L3_B": second(i["L3_ffn_B"]),
    }
    for n in ("q", "k", "v", "o"):
        d[f"L0_W{n}T"] = i[f"L0_xattn_W{n}"].T
    for n in ("L0_xattn_bq", "L0_xattn_bk", "L0_xattn_bv", "L0_xattn_bo", "L0_ffn_b_base", "L1_ffn_b_base",
              "L1_ffn_b_thr", "L3_ffn_br", "L2_ffn_b", "L3_xattn_q_norm_w", "L3_xattn_k_norm_w"):
        d[n] = i[n]
    d.update(constants())
    return {n: np.ascontiguousarray(z) for n, z in d.items()}


def kernel(**inputs):
    import concourse.bacc as bacc
    from concourse.bass_utils import run_bass_kernel_spmd

    nc = bacc.Bacc("TRN2", target_bir_lowering=False, num_devices=1)
    arrays, aps = {}, {}
    for name, z in layouts({n: np.asarray(v) for n, v in inputs.items()}).items():
        arrays[f"in_{name}"] = z
        aps[name] = nc.dram_tensor(f"in_{name}", z.shape, mybir.dt.from_np(z.dtype), kind="ExternalInput").ap()
    out = nc.dram_tensor("out_rows", (G, P, NT, D), F32, kind="ExternalOutput").ap()
    build(nc, aps, out)
    r = run_bass_kernel_spmd(nc, [arrays], core_ids=[0])
    return r.results[0]["out_rows"].transpose(0, 2, 1, 3).reshape(B, S, D)
```
